# Optimizing a Trainium2 kernel written in Bass

```python
import numpy as np
import jax
import jax.numpy as jnp

def _softmax(x, axis=-1):
    return jax.nn.softmax(x, axis=axis)

def _gelu(x):
    return jax.nn.gelu(x, approximate=True)

def _silu(x):
    return jax.nn.silu(x)

def _sigmoid(x):
    return jax.nn.sigmoid(x)

def _layernorm(x, axis=-1, eps=1e-05):
    m = jnp.mean(x, axis=axis, keepdims=True)
    v = jnp.var(x, axis=axis, keepdims=True)
    return (x - m) / jnp.sqrt(v + eps)

def _scatter_add(tgt, idx, src, axis=0):
    return tgt.at[idx].add(src)

def _segment_sum(src, seg, n):
    return jax.ops.segment_sum(src, seg, n)
kernel_name = 'mk_cond_seq_d2_seqx_r8_4ff1f2'

def setup_inputs(seed: int=0):
    np.random.seed(seed)
    _w = jnp.asarray

    def _rec_inputs():
        import jax
        import jax.numpy as jnp
        _rk = jax.random.key(seed)
        x = -0.0002928 + 1 * jax.random.normal(jax.random.fold_in(_rk, 1), (4, 256, 128), jnp.float32)
        _lenS = 256 - jax.random.randint(jax.random.fold_in(_rk, 7), (4,), 0, max(1, 256 // 4) + 1, jnp.int32)
        _lenS2 = 256 - jax.random.randint(jax.random.fold_in(_rk, 8), (4,), 0, max(1, 256 // 4) + 1, jnp.int32)
        itok_B_6_14 = jax.random.randint(jax.random.fold_in(_rk, 11), (4,), 6, 15, jnp.int32)
        condB_theta = jax.random.uniform(jax.random.fold_in(_rk, 12), (4,), jnp.float32, 0.0, 0.983423)
        condB_phi = jax.random.uniform(jax.random.fold_in(_rk, 13), (4,), jnp.float32, 0.0, 0.961312)
        return (x, itok_B_6_14, condB_theta, condB_phi)
    x, itok_B_6_14, condB_theta, condB_phi = _rec_inputs()

    def _L0_cond_setup():
        import jax, jax.numpy as jnp
        import numpy as np
        D = 128
        E = 8
        FF = 512
        TOPK = 2
        S = 32
        SE = 64
        SH = 128
        B, T = (2, 256)

        def _forward(x, subject_ids, ln_g, ln_b, subj_emb, hyp_w1, hyp_b1, hyp_w2, hyp_b2, sty_w1, sty_b1, sty_w2, sty_b2, router_w, exp_w1, exp_b1, exp_w2, exp_b2):
            mu = x.mean(-1, keepdims=True)
            var = x.var(-1, keepdims=True)
            h = (x - mu) * jax.lax.rsqrt(var + 1e-05) * ln_g + ln_b
            m_t = h.mean(1, keepdims=True)
            v_t = h.var(1, keepdims=True)
            h_norm = (h - m_t) * jax.lax.rsqrt(v_t + 1e-08)
            se = subj_emb[subject_ids]
            hyp = jax.nn.relu(se @ hyp_w1 + hyp_b1) @ hyp_w2 + hyp_b2
            sty = jax.nn.relu(hyp @ sty_w1 + sty_b1) @ sty_w2 + sty_b2
            gamma, beta = jnp.split(sty, 2, axis=-1)
            gamma = jax.nn.softplus(gamma) + 1e-08
            h = h_norm * gamma[:, None, :] + beta[:, None, :]
            h_flat = h.reshape(-1, D)
            probs = jax.nn.softmax(h_flat @ router_w, axis=-1)
            gates, idx = jax.lax.top_k(probs, TOPK)
            gates = gates / gates.sum(-1, keepdims=True)
            N = h_flat.shape[0]
            combine = jnp.zeros((N, E), h_flat.dtype).at[jnp.arange(N)[:, None], idx].add(gates)
            hid = jax.nn.relu(jnp.einsum('nd,edf->nef', h_flat, exp_w1) + exp_b1)
            eout = jnp.einsum('nef,efd->ned', hid, exp_w2) + exp_b2
            y = jnp.einsum('ned,ne->nd', eout, combine)
            return x + y.reshape(x.shape)
        key = jax.random.key(seed)
        ks = jax.random.split(key, 16)
        n = lambda k, sh, s=0.02: jax.random.normal(k, sh, dtype=jnp.float32) * s
        return {'x': jax.random.normal(ks[0], (B, T, D), dtype=jnp.float32), 'subject_ids': jax.random.randint(ks[1], (B,), 0, S), 'ln_g': jnp.ones((D,), jnp.float32), 'ln_b': jnp.zeros((D,), jnp.float32), 'subj_emb': n(ks[2], (S, SE)), 'hyp_w1': n(ks[3], (SE, SH), 1.0 / np.sqrt(SE)), 'hyp_b1': jnp.zeros((SH,), jnp.float32), 'hyp_w2': n(ks[4], (SH, SH), 1.0 / np.sqrt(SH)), 'hyp_b2': jnp.zeros((SH,), jnp.float32), 'sty_w1': n(ks[5], (SH, SH // 2), 1.0 / np.sqrt(SH)), 'sty_b1': jnp.zeros((SH // 2,), jnp.float32), 'sty_w2': n(ks[6], (SH // 2, 2 * D), 1.0 / np.sqrt(SH // 2)), 'sty_b2': jnp.zeros((2 * D,), jnp.float32), 'router_w': n(ks[7], (D, E), 1.0 / np.sqrt(D)), 'exp_w1': n(ks[8], (E, D, FF), 1.0 / np.sqrt(D)), 'exp_b1': jnp.zeros((E, FF), jnp.float32), 'exp_w2': n(ks[9], (E, FF, D), 1.0 / np.sqrt(FF)), 'exp_b2': jnp.zeros((E, D), jnp.float32)}
    _L0_cond_all = _L0_cond_setup()
    _L0_cond_in = {k: v for k, v in _L0_cond_all.items() if k in ('ln_g', 'ln_b', 'subj_emb', 'hyp_w1', 'hyp_b1', 'hyp_w2', 'hyp_b2', 'sty_w1', 'sty_b1', 'sty_w2', 'sty_b2', 'router_w', 'exp_w1', 'exp_b1', 'exp_w2', 'exp_b2')}
    del _L0_cond_all

    def _L1_cond_setup():
        import jax, jax.numpy as jnp
        import numpy as np
        key = jax.random.key(seed)
        k1, k2, k3 = jax.random.split(key, 3)
        B, N, D = (16, 512, 128)
        embeddings = jax.random.normal(k1, (B, N, D), dtype=jnp.float32)
        theta = jax.random.uniform(k2, (B,), dtype=jnp.float32)
        phi = jax.random.uniform(k3, (B,), dtype=jnp.float32)
        return {'embeddings': embeddings, 'theta': theta, 'phi': phi}
    _L1_cond_all = _L1_cond_setup()
    _L1_cond_in = {k: v for k, v in _L1_cond_all.items() if k in ()}
    del _L1_cond_all
    return {'x': x, 'itok_B_6_14': itok_B_6_14, 'condB_theta': condB_theta, 'condB_phi': condB_phi, 'L0_cond_ln_g': _L0_cond_in['ln_g'], 'L0_cond_ln_b': _L0_cond_in['ln_b'], 'L0_cond_subj_emb': _L0_cond_in['subj_emb'], 'L0_cond_hyp_w1': _L0_cond_in['hyp_w1'], 'L0_cond_hyp_b1': _L0_cond_in['hyp_b1'], 'L0_cond_hyp_w2': _L0_cond_in['hyp_w2'], 'L0_cond_hyp_b2': _L0_cond_in['hyp_b2'], 'L0_cond_sty_w1': _L0_cond_in['sty_w1'], 'L0_cond_sty_b1': _L0_cond_in['sty_b1'], 'L0_cond_sty_w2': _L0_cond_in['sty_w2'], 'L0_cond_sty_b2': _L0_cond_in['sty_b2'], 'L0_cond_router_w': _L0_cond_in['router_w'], 'L0_cond_exp_w1': _L0_cond_in['exp_w1'], 'L0_cond_exp_b1': _L0_cond_in['exp_b1'], 'L0_cond_exp_w2': _L0_cond_in['exp_w2'], 'L0_cond_exp_b2': _L0_cond_in['exp_b2']}

def reference(x, itok_B_6_14, condB_theta, condB_phi, L0_cond_ln_g, L0_cond_ln_b, L0_cond_subj_emb, L0_cond_hyp_w1, L0_cond_hyp_b1, L0_cond_hyp_w2, L0_cond_hyp_b2, L0_cond_sty_w1, L0_cond_sty_b1, L0_cond_sty_w2, L0_cond_sty_b2, L0_cond_router_w, L0_cond_exp_w1, L0_cond_exp_b1, L0_cond_exp_w2, L0_cond_exp_b2):
    import jax
    import jax.numpy as jnp

    def _L0_cond_ref(x, subject_ids, ln_g, ln_b, subj_emb, hyp_w1, hyp_b1, hyp_w2, hyp_b2, sty_w1, sty_b1, sty_w2, sty_b2, router_w, exp_w1, exp_b1, exp_w2, exp_b2):
        import jax, jax.numpy as jnp
        import numpy as np
        D = 128
        E = 8
        FF = 512
        TOPK = 2
        S = 32
        SE = 64
        SH = 128
        B, T = (2, 256)

        def _forward(x, subject_ids, ln_g, ln_b, subj_emb, hyp_w1, hyp_b1, hyp_w2, hyp_b2, sty_w1, sty_b1, sty_w2, sty_b2, router_w, exp_w1, exp_b1, exp_w2, exp_b2):
            mu = x.mean(-1, keepdims=True)
            var = x.var(-1, keepdims=True)
            h = (x - mu) * jax.lax.rsqrt(var + 1e-05) * ln_g + ln_b
            m_t = h.mean(1, keepdims=True)
            v_t = h.var(1, keepdims=True)
            h_norm = (h - m_t) * jax.lax.rsqrt(v_t + 1e-08)
            se = subj_emb[subject_ids]
            hyp = jax.nn.relu(se @ hyp_w1 + hyp_b1) @ hyp_w2 + hyp_b2
            sty = jax.nn.relu(hyp @ sty_w1 + sty_b1) @ sty_w2 + sty_b2
            gamma, beta = jnp.split(sty, 2, axis=-1)
            gamma = jax.nn.softplus(gamma) + 1e-08
            h = h_norm * gamma[:, None, :] + beta[:, None, :]
            h_flat = h.reshape(-1, D)
            probs = jax.nn.softmax(h_flat @ router_w, axis=-1)
            gates, idx = jax.lax.top_k(probs, TOPK)
            gates = gates / gates.sum(-1, keepdims=True)
            N = h_flat.shape[0]
            combine = jnp.zeros((N, E), h_flat.dtype).at[jnp.arange(N)[:, None], idx].add(gates)
            hid = jax.nn.relu(jnp.einsum('nd,edf->nef', h_flat, exp_w1) + exp_b1)
            eout = jnp.einsum('nef,efd->ned', hid, exp_w2) + exp_b2
            y = jnp.einsum('ned,ne->nd', eout, combine)
            return x + y.reshape(x.shape)
        return _forward(x, subject_ids, ln_g, ln_b, subj_emb, hyp_w1, hyp_b1, hyp_w2, hyp_b2, sty_w1, sty_b1, sty_w2, sty_b2, router_w, exp_w1, exp_b1, exp_w2, exp_b2)

    def _L1_cond_ref(embeddings, theta, phi):
        import jax, jax.numpy as jnp
        import numpy as np
        B, N, D = embeddings.shape
        e = embeddings.reshape(B, N, D // 4, 4)
        ct = jnp.cos(theta)[:, None, None]
        st = jnp.sin(theta)[:, None, None]
        cp = jnp.cos(phi)[:, None, None]
        sp = jnp.sin(phi)[:, None, None]
        x0, x1, x2, x3 = (e[..., 0], e[..., 1], e[..., 2], e[..., 3])
        out = jnp.stack([x0 * ct + x1 * st, -x0 * st + x1 * ct, x2 * cp + x3 * sp, -x2 * sp + x3 * cp], axis=-1)
        return out.reshape(B, N, D)
    x = _L0_cond_ref(x, itok_B_6_14, L0_cond_ln_g, L0_cond_ln_b, L0_cond_subj_emb, L0_cond_hyp_w1, L0_cond_hyp_b1, L0_cond_hyp_w2, L0_cond_hyp_b2, L0_cond_sty_w1, L0_cond_sty_b1, L0_cond_sty_w2, L0_cond_sty_b2, L0_cond_router_w, L0_cond_exp_w1, L0_cond_exp_b1, L0_cond_exp_w2, L0_cond_exp_b2)
    x = _L1_cond_ref(x, condB_theta, condB_phi)
    return x

_drawn_inputs = setup_inputs


def setup_inputs(seed=0):
    import zlib

    import numpy as np

    out = dict(_drawn_inputs(seed))
    spreads = {'L0_cond_ln_g': (1.0, 0.2),
     'L0_cond_ln_b': (0.0, 0.1),
     'L0_cond_hyp_b1': (0.0, 0.1),
     'L0_cond_hyp_b2': (0.0, 0.1),
     'L0_cond_sty_b1': (0.0, 0.1),
     'L0_cond_sty_b2': (0.0, 0.1),
     'L0_cond_exp_b1': (0.0, 0.1),
     'L0_cond_exp_b2': (0.0, 0.1)}
    factors = {}
    for name, (base, spread) in spreads.items():
        noise = np.random.default_rng([zlib.crc32(name.encode()), seed]).standard_normal(out[name].shape)
        drawn = base * np.exp(spread * noise) if base else spread * noise
        out[name] = jnp.asarray(drawn.astype(out[name].dtype))
    for name, factor in factors.items():
        out[name] = (out[name] * factor).astype(out[name].dtype)
    return out
```

```python
from contextlib import ExitStack

import concourse.bass as bass
from concourse import mybir

ALU = mybir.AluOpType
ACT = mybir.ActivationFunctionType
F32 = mybir.dt.float32
F32R = mybir.dt.float32r
I32 = mybir.dt.int32
U32 = mybir.dt.uint32

P = 128
B = 4
T = 256
D = 128
E = 8
FF = 512
C = FF // P
NT = B * T // P
HALF = 512
TH = HALF // P
N = B * T
SUBJECTS, SE, SH = 32, 64, 128
UNITS = 2 * C
PASS = 2 * UNITS
WCOLS = FF + C * D

IDENT, PARTNER = 0, 128
(LN_G, LN_B, HYP_B1, HYP_B2, STY_B1, STY_BG, STY_BB) = range(256, 263)
ANGLE = 263
ROUTER = ANGLE + B
EXPERT_NO = ROUTER + E
NPAR = EXPERT_NO + E
HYP_W2, STY_W1, HYP_W1, STY_W2, SUBJ, EXP_B2 = 0, 128, 192, 320, 576, 640
NSUB = 768

LN_EPS, TIME_EPS, GAMMA_EPS = 1e-5, 1e-8, 1e-8
TWO_PI_HI = 6.28125
TWO_PI_LO = 0.0019353071795864769
ROUND = 12582912.0
PI_BELOW = 3.1415925
HALF_PI = 1.5707963267948966


def moe_rotate(nc, x, itok, params, subnet, experts, exp_b1, out):
    with ExitStack() as ctx:
        def sb(name, shape, dt=F32):
            return ctx.enter_context(nc.sbuf_tensor(name, shape, dt))

        def sem(name):
            return ctx.enter_context(nc.semaphore(name))

        par = sb("par", [P, NPAR])
        sub = sb("sub", [P, NSUB])
        itok_i = sb("itok_i", [SUBJECTS, B], I32)
        itok_f = sb("itok_f", [SUBJECTS, B])
        row_no = sb("row_no", [SUBJECTS, 1])
        onehot = sb("onehot", [SUBJECTS, B])
        consts = sb("consts", [P, 4])
        eps_ln, eps_time, one, half_pi = (consts[:, i:i + 1] for i in range(4))
        x_tok = sb("x_tok", [P, NT, D])
        z_tok = sb("z_tok", [P, NT, D])
        out_tok = sb("out_tok", [P, NT, D])
        tok_part = sb("tok_part", [P, NT, 6])
        tok_stat = sb("tok_stat", [P, NT, 2])
        tok_ln = sb("tok_ln", [P, NT])
        tok_guess = sb("tok_guess", [P, NT])
        tok_tmp = sb("tok_tmp", [P, 3, NT])
        tok_rstd = sb("tok_rstd", [P, NT])
        h = sb("h", [P, N])
        feat_part = sb("feat_part", [P, B, 6])
        feat_stat = sb("feat_stat", [P, B, 2])
        feat_ln = sb("feat_ln", [P, B])
        feat_guess = sb("feat_guess", [P, B])
        feat_tmp = sb("feat_tmp", [P, 3, B])
        feat_rstd = sb("feat_rstd", [P, B])
        feat_scale = sb("feat_scale", [P, B])
        scaled = sb("scaled", [P, N])
        x_hi = sb("x_hi", [P, N], F32R)
        x_lo = sb("x_lo", [P, N], F32R)
        emb = sb("emb", [SE, B])
        hyp1 = sb("hyp1", [SH, B])
        hyp = sb("hyp", [SH, B])
        sty1 = sb("sty1", [SH // 2, B])
        gamma_raw = sb("gamma_raw", [P, B])
        beta = sb("beta", [P, B])
        sp_abs = sb("sp_abs", [P, B])
        sp_exp = sb("sp_exp", [P, B])
        sp_ln = sb("sp_ln", [P, B])
        sp_one = sb("sp_one", [P, B])
        sp_err = sb("sp_err", [P, B])
        sp_log1p = sb("sp_log1p", [P, B])
        gamma = sb("gamma", [P, B])
        router_hi = sb("router_hi", [P, E], F32R)
        router_lo = sb("router_lo", [P, E], F32R)
        logit_rows = sb("logit_rows", [E, N])
        logits = sb("logits", [P, NT, E])
        top = sb("top", [P, NT, 8])
        top_at = sb("top_at", [P, NT, 8], U32)
        top_at_f = sb("top_at_f", [P, NT, 2])
        gap = sb("gap", [P, NT])
        gap_exp = sb("gap_exp", [P, NT])
        gap_sum = sb("gap_sum", [P, NT])
        gates = sb("gates", [P, NT, 2])
        picked = sb("picked", [P, 2, NT, E])
        combine = sb("combine", [P, NT, E])
        combine_rows = sb("combine_rows", [E, N])
        w_raw = [sb(f"w_raw{i}", [P, WCOLS]) for i in range(2)]
        w_hi = [sb(f"w_hi{i}", [P, WCOLS], F32R) for i in range(2)]
        w_lo = [sb(f"w_lo{i}", [P, WCOLS], F32R) for i in range(2)]
        b1 = [sb(f"b1_{i}", [P, C]) for i in range(2)]
        gate_all = [sb(f"gate_all{i}", [P, N]) for i in range(2)]
        hid = [sb(f"hid{i}", [P, HALF]) for i in range(4)]
        hid_hi = [sb(f"hid_hi{i}", [P, HALF], F32R) for i in range(4)]
        hid_lo = [sb(f"hid_lo{i}", [P, HALF], F32R) for i in range(4)]
        gated = [sb(f"gated{i}", [P, HALF]) for i in range(2)]
        acc = [sb(f"acc{i}", [P, HALF]) for i in range(2)]
        angle = sb("angle", [P, 4, B])
        sin_a = sb("sin_a", [P, B])
        cos_a = sb("cos_a", [P, B])
        rot_tmp = sb("rot_tmp", [P, 2, B, D])
        rotation = sb("rotation", [P, B, D])

        ps_hid = [ctx.enter_context(nc.psum_tensor(f"ps_hid{i}", [P, HALF], F32)) for i in range(4)]
        ps_out = [ctx.enter_context(nc.psum_tensor(f"ps_out{i}", [P, HALF], F32)) for i in range(2)]
        ps_aux = [ctx.enter_context(nc.psum_tensor(f"ps_aux{i}", [P, HALF], F32)) for i in range(2)]

        ps_final = [*ps_aux, *ps_hid[:2]]

        gate_dram = nc.dram_tensor("gate_dram", [E, N], F32, kind="Internal").ap()

        x_in = [sem(f"x_in{b}") for b in range(B)]
        par_in, sub_in, itok_in = sem("par_in"), sem("sub_in"), sem("itok_in")
        w_in = [sem(f"w_in{i}") for i in range(2)]
        b1_in = [sem(f"b1_in{i}") for i in range(2)]
        gate_in = [sem(f"gate_in{i}") for i in range(2)]
        gate_out = sem("gate_out")
        out_done = sem("out_done")
        pool_step = sem("pool_step")
        onehot_done, consts_done, angle_done, rotation_done = (
            sem("onehot_done"), sem("consts_done"), sem("angle_done"), sem("rotation_done"))
        w_lo0_done = sem("w_lo0_done")
        pe_raw, pe_z, pe_mlp = sem("pe_raw"), sem("pe_z"), sem("pe_mlp")
        pe_logit_rows, pe_logits, pe_gates, pe_b2, pe_final = (
            sem("pe_logit_rows"), sem("pe_logits"), sem("pe_gates"), sem("pe_b2"), sem("pe_final"))
        layer1_done, layer2_done = sem("layer1_done"), sem("layer2_done")
        raw_copied, mlp_copied = sem("raw_copied"), sem("mlp_copied")
        act_step = sem("act_step")
        tok_guessed, feat_guessed, h_done, x_hi_done = (
            sem("tok_guessed"), sem("feat_guessed"), sem("h_done"), sem("x_hi_done"))
        softplus_parts, gap_exp_done = sem("softplus_parts"), sem("gap_exp_done")
        logit_rows_copied, gates_copied = sem("logit_rows_copied"), sem("gates_copied")
        w_hi_done, w_lo_done = sem("w_hi_done"), sem("w_lo_done")
        act_done, hi_done, lo_done = sem("act_done"), sem("hi_done"), sem("lo_done")
        trig_done, out_copied = sem("trig_done"), sem("out_copied")
        dve_step = sem("dve_step")
        tok_stats, feat_stats, z_done, scaled_done, x_lo_done = (
            sem("tok_stats"), sem("feat_stats"), sem("z_done"), sem("scaled_done"), sem("x_lo_done"))
        router_done, logits_copied, gap_done, combine_done, acc_started = (
            sem("router_done"), sem("logits_copied"), sem("gap_done"), sem("combine_done"), sem("acc_started"))
        gated_done, acc_done = sem("gated_done"), sem("acc_done")

        x_view = x.rearrange("b (p j) d -> b p (j d)", p=P)
        out_view = out.rearrange("b (p j) d -> b p (j d)", p=P)
        ident = par[:, IDENT:IDENT + P]

        def w1(w, c):
            return w[:, c * P:(c + 1) * P]

        def w2(w, c):
            return w[:, FF + c * D:FF + (c + 1) * D]

        def half(a, n):
            return a[:, n * HALF:(n + 1) * HALF]

        block = ctx.enter_context(nc.Block())

        @block.sync
        def _(sp):
            for b in (0, 1):
                nc.sync.dma_start(x_tok[:, 2 * b:2 * b + 2, :].rearrange("p j d -> p (j d)"), x_view[b]).then_inc(x_in[b], 16)
            nc.sync.dma_start(w_raw[0][:], experts[0]).then_inc(w_in[0], 16)
            nc.sync.dma_start(b1[0][:], exp_b1[0]).then_inc(b1_in[0], 16)
            nc.sync.dma_start(b1[1][:], exp_b1[1]).then_inc(b1_in[1], 16)
            nc.sync.dma_start(w_raw[1][:], experts[1]).then_inc(w_in[1], 16)
            sp.wait_ge(gates_copied, 2)
            nc.sync.dma_start(gate_dram, combine_rows[:]).then_inc(gate_out, 16)
            sp.wait_ge(gate_out, 16)
            for e in (0, 1):
                nc.sync.dma_start(gate_all[e][:], gate_dram[e:e + 1, :].partition_broadcast(P)).then_inc(gate_in[e], 16)

            def prefetch(i, s, weights=True, more=True):
                e = 2 * i + s
                if more:
                    sp.wait_ge(act_done, UNITS * e)
                    nc.sync.dma_start(b1[1 - s][:], exp_b1[bass.ds(e + 1, 1)].rearrange("e p c -> (e p) c")).then_inc(b1_in[1 - s], 16)
                    sp.wait_ge(gated_done, 2 * e)
                    nc.sync.dma_start(gate_all[1 - s][:], gate_dram[bass.ds(e + 1, 1), :].partition_broadcast(P)).then_inc(gate_in[1 - s], 16)
                if weights:
                    sp.wait_ge(w_lo_done, e + 1)
                    nc.sync.dma_start(w_raw[s][:], experts[bass.ds(e + 2, 1)].rearrange("e p c -> (e p) c")).then_inc(w_in[s], 16)

            prefetch(0, 0, more=False)
            prefetch(0, 1)
            with sp.Fori(1, 3) as i:
                prefetch(i, 0)
                prefetch(i, 1)
            prefetch(3, 0, weights=False)
            for b in (0, 1):
                sp.wait_ge(out_copied, b + 1)
                nc.sync.dma_start(out_view[b], out_tok[:, 2 * b:2 * b + 2, :].rearrange("p j d -> p (j d)")).then_inc(out_done, 16)
            sp.wait_ge(out_copied, 3)
            nc.sync.dma_start(out_view[2], out_tok[:, 4:6, :].rearrange("p j d -> p (j d)")).then_inc(out_done, 16)
            sp.wait_ge(out_done, 16 * B)

        @block.gpsimd
        def _(pool):
            steps = [0]

            def link(ins):
                steps[0] += 1
                ins.then_inc(pool_step, 1)
                pool.wait_ge(pool_step, steps[0])

            nc.gpsimd.dma_start(itok_i[:], itok.rearrange("(o b) -> o b", o=1).partition_broadcast(SUBJECTS)).then_inc(itok_in, 16)
            nc.gpsimd.memset(eps_ln, LN_EPS)
            nc.gpsimd.memset(eps_time, TIME_EPS)
            nc.gpsimd.memset(one, 1.0)
            nc.gpsimd.memset(half_pi, HALF_PI).then_inc(consts_done, 1)
            link(nc.gpsimd.iota(row_no[:], [[0, 1]], base=0, channel_multiplier=1, allow_small_or_imprecise_dtypes=True))
            pool.wait_ge(itok_in, 16)
            link(nc.gpsimd.tensor_copy(itok_f[:], itok_i[:]))
            nc.gpsimd.tensor_scalar(onehot[:], itok_f[:], row_no[:, 0:1], None, ALU.is_equal).then_inc(onehot_done, 1)
            pool.wait_ge(par_in, 16)
            a = par[:, ANGLE:ANGLE + B]
            link(nc.gpsimd.tensor_scalar(angle[:, 0, :], a, 0.15915494309189535, ROUND, ALU.mult, ALU.add))
            link(nc.gpsimd.tensor_scalar(angle[:, 0, :], angle[:, 0, :], ROUND, None, ALU.subtract))
            link(nc.gpsimd.tensor_scalar(angle[:, 1, :], angle[:, 0, :], TWO_PI_HI, None, ALU.mult))
            link(nc.gpsimd.tensor_scalar(angle[:, 2, :], angle[:, 0, :], TWO_PI_LO, None, ALU.mult))
            link(nc.gpsimd.tensor_tensor(angle[:, 3, :], a, angle[:, 1, :], ALU.subtract))
            link(nc.gpsimd.tensor_tensor(angle[:, 1, :], angle[:, 3, :], angle[:, 2, :], ALU.subtract))
            nc.gpsimd.tensor_scalar(angle[:, 0, :], angle[:, 1, :], PI_BELOW, -PI_BELOW, ALU.min, ALU.max).then_inc(angle_done, 1)
            pool.wait_ge(w_hi_done, 1)
            nc.gpsimd.tensor_tensor(w_lo[0][:], w_raw[0][:], w_hi[0][:].bitcast(F32), ALU.subtract).then_inc(w_lo_done, 1)
            pool.wait_ge(trig_done, 1)
            for b in range(B):
                nc.gpsimd.tensor_scalar(rot_tmp[:, 0, b, :], ident, cos_a[:, b:b + 1], None, ALU.mult)
                link(nc.gpsimd.tensor_scalar(rot_tmp[:, 1, b, :], par[:, PARTNER:PARTNER + D], sin_a[:, b:b + 1], None, ALU.mult))
            nc.gpsimd.tensor_tensor(rotation[:], rot_tmp[:, 0], rot_tmp[:, 1], ALU.add).then_inc(rotation_done, 1)

        @block.scalar
        def _(act):
            nc.scalar.dma_start(par[:], params).then_inc(par_in, 16)
            nc.scalar.dma_start(sub[:], subnet).then_inc(sub_in, 16)
            for b in (2, 3):
                nc.scalar.dma_start(x_tok[:, 2 * b:2 * b + 2, :].rearrange("p j d -> p (j d)"), x_view[b]).then_inc(x_in[b], 16)
            nc.scalar.preload_act_table_set("natural_log_exp_and_others")
            steps = [0]

            def link(ins):
                steps[0] += 1
                ins.then_inc(act_step, 1)
                act.wait_ge(act_step, steps[0])

            def copy_x_features(n):
                act.wait_ge(pe_raw, n + 1)
                nc.scalar.copy(acc[n][:], ps_aux[n][:]).then_inc(raw_copied, 1)

            def guess(n, stat, eps, ln, first, width, ready, done):
                act.wait_ge(ready, n + 1)
                s = slice(n * width, (n + 1) * width)
                link(nc.scalar.activation(ln[:, s], stat[:, s, 1], ACT.Ln, bias=eps))
                nc.scalar.activation(first[:, s], ln[:, s], ACT.Exp, scale=-0.5).then_inc(done, 1)

            def mlp(k, dst, rows, func, bias):
                act.wait_ge(pe_mlp, k + 1)
                src = ps_hid[k // 5][0:rows, 8 * k:8 * k + B]
                if bias is None:
                    ins = nc.scalar.copy(dst[:], src)
                else:
                    ins = nc.scalar.activation(dst[:], src, func, bias=par[0:rows, bias:bias + 1])
                ins.then_inc(mlp_copied, 1)

            def affine(n):
                act.wait_ge(pe_z, n + 1)
                nc.scalar.activation(half(h, n), ps_out[n][:], ACT.Identity, bias=par[:, LN_B:LN_B + 1],
                                     scale=par[:, LN_G:LN_G + 1]).then_inc(h_done, 1)

            def high_x(b):
                act.wait_ge(scaled_done, b + 1)
                s = slice(b * T, (b + 1) * T)
                nc.scalar.activation(x_hi[:, s], scaled[:, s], ACT.Identity, bias=beta[:, b:b + 1]).then_inc(x_hi_done, 1)

            def high_weights(e, s):
                act.wait_ge(w_in[s], 16 * (e // 2 + 1) if isinstance(e, int) else e)
                nc.scalar.copy(w_hi[s][:], w_raw[s][:]).then_inc(w_hi_done, 1)

            act.wait_ge(consts_done, 1)
            act.wait_ge(par_in, 16)
            copy_x_features(0)
            mlp(0, emb, SE, None, None)
            mlp(1, hyp1, SH, ACT.Relu, HYP_B1)
            guess(0, tok_stat, eps_ln, tok_ln, tok_guess, TH, tok_stats, tok_guessed)
            mlp(2, hyp, SH, ACT.Identity, HYP_B2)
            copy_x_features(1)
            affine(0)
            mlp(3, sty1, SH // 2, ACT.Relu, STY_B1)
            guess(1, tok_stat, eps_ln, tok_ln, tok_guess, TH, tok_stats, tok_guessed)
            mlp(4, gamma_raw, P, ACT.Identity, STY_BG)
            mlp(5, beta, P, ACT.Identity, STY_BB)
            act.wait_ge(mlp_copied, 6)
            link(nc.scalar.activation(sp_abs[:], gamma_raw[:], ACT.Abs))
            link(nc.scalar.activation(sp_exp[:], sp_abs[:], ACT.Exp, scale=-1.0))
            nc.scalar.activation(sp_ln[:], sp_exp[:], ACT.Ln, bias=one).then_inc(softplus_parts, 1)
            guess(0, feat_stat, eps_time, feat_ln, feat_guess, 2, feat_stats, feat_guessed)
            act.wait_ge(w_in[0], 16)
            nc.scalar.copy(w_hi[0][:], w_raw[0][:]).then_inc(w_hi_done, 1)
            affine(1)
            high_x(0)
            high_x(1)
            guess(1, feat_stat, eps_time, feat_ln, feat_guess, 2, feat_stats, feat_guessed)
            high_x(2)
            high_x(3)

            def unit(i, k, first=False, split_next=True):
                s, q = k // UNITS, k % 4
                u = PASS * i + k
                if k % UNITS == 0:
                    act.wait_ge(b1_in[s], 16 * (i + 1))
                act.wait_ge(layer1_done, u + 1)
                bias = b1[s][:, k % C:k % C + 1]
                if q != 3:
                    if not (first and k < 4):
                        act.wait_ge(layer2_done, u - 3)
                    nc.scalar.activation(hid_hi[q][:], ps_hid[q][:], ACT.Relu, bias=bias)
                if not (first and k < 4):
                    act.wait_ge(lo_done, u - 3)
                nc.scalar.activation(hid[q][:], ps_hid[q][:], ACT.Relu, bias=bias).then_inc(act_done, 1)
                if k % UNITS == 3 and split_next:
                    n = 1 - s
                    act.wait_ge(w_in[n], 16 * (i + 1 + s))
                    if not (first and s == 0):
                        act.wait_ge(layer2_done, PASS * i + s * UNITS)
                    nc.scalar.copy(w_hi[n][:], w_raw[n][:]).then_inc(w_hi_done, 1)

            for k in range(PASS):
                unit(0, k, first=True)
                if k == 0:
                    for n in range(2):
                        act.wait_ge(pe_logit_rows, n + 1)
                        nc.scalar.copy(logit_rows[:, n * HALF:(n + 1) * HALF], ps_aux[n][0:E, :]).then_inc(logit_rows_copied, 1)
                if k == 3:
                    act.wait_ge(gap_done, 1)
                    nc.scalar.activation(gap_exp[:], gap[:], ACT.Exp).then_inc(gap_exp_done, 1)
                if k == 5:
                    for n in range(2):
                        act.wait_ge(pe_gates, n + 1)
                        nc.scalar.copy(combine_rows[:, n * HALF:(n + 1) * HALF], ps_aux[n][0:E, :]).then_inc(gates_copied, 1)
                if k == 12:
                    act.wait_ge(angle_done, 1)
                    nc.scalar.activation(sin_a[:], angle[:, 0, :], ACT.Sin)
                    link(nc.scalar.activation(angle[:, 1, :], angle[:, 0, :], ACT.Abs))
                    nc.scalar.activation(cos_a[:], angle[:, 1, :], ACT.Sin, bias=half_pi, scale=-1.0).then_inc(trig_done, 1)
            with act.Fori(1, 3) as i:
                for k in range(PASS):
                    unit(i, k)
            for k in range(PASS):
                unit(3, k, split_next=k < UNITS)
            for b in range(B):
                act.wait_ge(pe_final, b + 1)
                nc.scalar.copy(out_tok[:, 2 * b:2 * b + 2, :].rearrange("p j d -> p (j d)"),
                               ps_final[b][:, 0:2 * D]).then_inc(out_copied, 1)
            act.wait_ge(out_copied, 4)
            nc.scalar.dma_start(out_view[3], out_tok[:, 6:8, :].rearrange("p j d -> p (j d)")).then_inc(out_done, 16)

        @block.vector
        def _(dve):
            steps = [0]

            def link(ins):
                steps[0] += 1
                ins.then_inc(dve_step, 1)
                dve.wait_ge(dve_step, steps[0])

            def token_stats(n):
                for t in range(n * TH, (n + 1) * TH):
                    if t % 2 == 0:
                        dve.wait_ge(x_in[t // 2], 16)
                    ins = nc.vector.bn_stats(tok_part[:, t, :], x_tok[:, t, :])
                link(ins)
                for t in range(n * TH, (n + 1) * TH):
                    ins = nc.vector.bn_aggr(tok_stat[:, t, :], tok_part[:, t, :])
                ins.then_inc(tok_stats, 1)

            def refine(n, stat, eps, first, tmp, rstd, width, guessed):
                s = slice(n * width, (n + 1) * width)
                dve.wait_ge(guessed, n + 1)
                link(nc.vector.tensor_tensor(tmp[:, 0, s], first[:, s], first[:, s], ALU.mult))
                link(nc.vector.scalar_tensor_tensor(tmp[:, 1, s], stat[:, s, 1], eps, tmp[:, 0, s], ALU.add, ALU.mult))
                link(nc.vector.tensor_scalar(tmp[:, 2, s], tmp[:, 1, s], -0.5, 1.5, ALU.mult, ALU.add))
                link(nc.vector.tensor_tensor(rstd[:, s], tmp[:, 2, s], first[:, s], ALU.mult))

            def normalise(n):
                for t in range(n * TH, (n + 1) * TH):
                    ins = nc.vector.tensor_scalar(z_tok[:, t, :], x_tok[:, t, :], tok_stat[:, t, 0:1], tok_rstd[:, t:t + 1],
                                                  ALU.subtract, ALU.mult)
                ins.then_inc(z_done, 1)

            def feature_stats(n):
                dve.wait_ge(h_done, n + 1)
                for b in (2 * n, 2 * n + 1):
                    ins = nc.vector.bn_stats(feat_part[:, b, :], h[:, b * T:(b + 1) * T])
                link(ins)
                for b in (2 * n, 2 * n + 1):
                    ins = nc.vector.bn_aggr(feat_stat[:, b, :], feat_part[:, b, :])
                ins.then_inc(feat_stats, 1)

            def style(n):
                s = slice(2 * n, 2 * n + 2)
                link(nc.vector.scalar_tensor_tensor(feat_scale[:, s], gamma[:, s], GAMMA_EPS, feat_rstd[:, s], ALU.add, ALU.mult))
                for b in (2 * n, 2 * n + 1):
                    c = slice(b * T, (b + 1) * T)
                    nc.vector.tensor_scalar(scaled[:, c], h[:, c], feat_stat[:, b, 0:1], feat_scale[:, b:b + 1],
                                            ALU.subtract, ALU.mult).then_inc(scaled_done, 1)

            def low_x(n):
                for b in (2 * n, 2 * n + 1):
                    c = slice(b * T, (b + 1) * T)
                    dve.wait_ge(x_hi_done, b + 1)
                    dve.wait_ge(scaled_done, b + 1)
                    ins = nc.vector.scalar_tensor_tensor(x_lo[:, c], scaled[:, c], beta[:, b:b + 1], x_hi[:, c].bitcast(F32),
                                                         ALU.add, ALU.subtract)
                ins.then_inc(x_lo_done, 1)

            token_stats(0)
            token_stats(1)
            refine(0, tok_stat, eps_ln, tok_guess, tok_tmp, tok_rstd, TH, tok_guessed)
            normalise(0)
            refine(1, tok_stat, eps_ln, tok_guess, tok_tmp, tok_rstd, TH, tok_guessed)
            normalise(1)
            feature_stats(0)
            dve.wait_ge(softplus_parts, 1)
            link(nc.vector.tensor_scalar(sp_one[:], sp_exp[:], 1.0, None, ALU.add))
            link(nc.vector.scalar_tensor_tensor(sp_err[:], sp_one[:], -1.0, sp_exp[:], ALU.add, ALU.subtract))
            link(nc.vector.tensor_tensor(sp_log1p[:], sp_ln[:], sp_err[:], ALU.subtract))
            link(nc.vector.scalar_tensor_tensor(gamma[:], gamma_raw[:], 0.0, sp_log1p[:], ALU.max, ALU.add))
            refine(0, feat_stat, eps_time, feat_guess, feat_tmp, feat_rstd, 2, feat_guessed)
            style(0)
            feature_stats(1)
            low_x(0)
            dve.wait_ge(par_in, 16)
            link(nc.vector.tensor_copy(router_hi[:], par[:, ROUTER:ROUTER + E]))
            nc.vector.tensor_tensor(router_lo[:], par[:, ROUTER:ROUTER + E], router_hi[:].bitcast(F32), ALU.subtract).then_inc(router_done, 1)
            refine(1, feat_stat, eps_time, feat_guess, feat_tmp, feat_rstd, 2, feat_guessed)
            style(1)
            low_x(1)

            def pick_experts():
                dve.wait_ge(pe_logits, 1)
                link(nc.vector.tensor_copy(logits[:].rearrange("p t e -> p (t e)"), ps_aux[0][:, 0:NT * E]))
                for t in range(NT):
                    ins = nc.vector.max(top[:, t, :], logits[:, t, :])
                link(ins)
                nc.vector.tensor_tensor(gap[:], top[:, :, 1], top[:, :, 0], ALU.subtract).then_inc(gap_done, 1)
                for t in range(NT):
                    ins = nc.vector.max_index(top_at[:, t, :], top[:, t, :], logits[:, t, :])
                link(ins)
                link(nc.vector.tensor_copy(top_at_f[:], top_at[:, :, 0:2]))
                numbers = par[:, EXPERT_NO:EXPERT_NO + E].unsqueeze(1).to_broadcast([P, NT, E])
                for j in range(2):
                    nc.vector.tensor_tensor(picked[:, j], numbers, top_at_f[:, :, j:j + 1].to_broadcast([P, NT, E]),
                                            ALU.is_equal).then_inc(dve_step, 1)
                    steps[0] += 1

            def weigh_experts():
                dve.wait_ge(gap_exp_done, 1)
                link(nc.vector.tensor_scalar(gap_sum[:], gap_exp[:], 1.0, None, ALU.add))
                link(nc.vector.reciprocal(gates[:, :, 0], gap_sum[:]))
                link(nc.vector.tensor_tensor(gates[:, :, 1], gap_exp[:], gates[:, :, 0], ALU.mult))
                for j in range(2):
                    ins = nc.vector.tensor_tensor(picked[:, j], picked[:, j], gates[:, :, j:j + 1].to_broadcast([P, NT, E]), ALU.mult)
                link(ins)
                nc.vector.tensor_tensor(combine[:], picked[:, 0], picked[:, 1], ALU.add).then_inc(combine_done, 1)

            def start_sum():
                for n in range(2):
                    dve.wait_ge(pe_b2, n + 1)
                    ins = nc.vector.tensor_tensor(acc[n][:], ps_aux[n][:], acc[n][:], ALU.add)
                link(ins)

            def gate_output(i, k, g):
                s, n = g // 2, g % 2
                dve.wait_ge(layer2_done, PASS * i + C * (g + 1))
                if n == 0:
                    dve.wait_ge(gate_in[s], 16 * (i + 1))
                nc.vector.tensor_tensor(gated[n][:], ps_out[n][:], half(gate_all[s], n), ALU.mult).then_inc(gated_done, 1)

            def add_output(i, g):
                n = g % 2
                dve.wait_ge(gated_done, 4 * i + g + 1)
                nc.vector.tensor_tensor(acc[n][:], acc[n][:], gated[n][:], ALU.add).then_inc(acc_done, 1)

            def unit(i, k, first=False, split_next=True):
                s, q = k // UNITS, k % 4
                u = PASS * i + k
                dve.wait_ge(act_done, u + 1)
                if not (first and k < 4):
                    dve.wait_ge(layer2_done, u - 3)
                if q == 3:
                    nc.vector.tensor_copy(hid_hi[q][:], hid[q][:]).then_inc(hi_done, 1)
                    dve.wait_ge(hi_done, 4 * i + k // 4 + 1)
                nc.vector.tensor_tensor(hid_lo[q][:], hid[q][:], hid_hi[q][:].bitcast(F32), ALU.subtract).then_inc(lo_done, 1)
                if k % UNITS == 4 and split_next:
                    n = 1 - s
                    dve.wait_ge(w_hi_done, 2 * i + s + 2)
                    nc.vector.tensor_tensor(w_lo[n][:], w_raw[n][:], w_hi[n][:].bitcast(F32), ALU.subtract).then_inc(w_lo_done, 1)

            def group_end(i, k, first=False):
                if first and k < 5:
                    return
                if k % 4 == 1:
                    g = k // 4 - 1
                    gate_output(*((i, k, g) if g >= 0 else (i - 1, k, 3)))
                if k % 4 == 2:
                    g = k // 4 - 1
                    add_output(*((i, g) if g >= 0 else (i - 1, 3)))

            for k in range(PASS):
                unit(0, k, first=True)
                if k == 1:
                    pick_experts()
                if k == 3:
                    weigh_experts()
                if k == 8:
                    start_sum()
                    gate_output(0, k, 0)
                if k == 9:
                    add_output(0, 0)
                    gate_output(0, k, 1)
                if k == 10:
                    add_output(0, 1)
                if k > 10:
                    group_end(0, k, first=True)
            with dve.Fori(1, 3) as i:
                for k in range(PASS):
                    unit(i, k)
                    group_end(i, k)
            for k in range(PASS):
                unit(3, k, split_next=k < UNITS)
                group_end(3, k)
            gate_output(3, PASS, 3)
            add_output(3, 3)

        @block.tensor
        def _(pe):
            def raw_transposes(n):
                for b in (2 * n, 2 * n + 1):
                    pe.wait_ge(x_in[b], 16)
                for j in range(TH):
                    ins = nc.tensor.transpose(ps_aux[n][:, j * P:(j + 1) * P], x_tok[:, n * TH + j, :], ident)
                ins.then_inc(pe_raw, 1)

            def z_transposes(n):
                pe.wait_ge(z_done, n + 1)
                for j in range(TH):
                    ins = nc.tensor.transpose(ps_out[n][:, j * P:(j + 1) * P], z_tok[:, n * TH + j, :], ident)
                ins.then_inc(pe_z, 1)

            def mlp(k, rows, weight, moving, need):
                if need:
                    pe.wait_ge(mlp_copied, need)
                nc.tensor.matmul(ps_hid[k // 5][0:rows, 8 * k:8 * k + B], weight, moving, start=True, stop=True).then_inc(pe_mlp, 1)

            def split_product(out_, hi, lo, moving_hi, moving_lo, start, stop):
                nc.tensor.matmul(out_, hi, moving_hi, start=start, stop=False)
                nc.tensor.matmul(out_, hi, moving_lo, start=False, stop=False)
                return nc.tensor.matmul(out_, lo, moving_hi, start=False, stop=stop)

            def logit_rows_of(n):
                pe.wait_ge(x_lo_done, n + 1)
                pe.wait_ge(raw_copied, n + 1)
                split_product(ps_aux[n][0:E, :], router_hi[:], router_lo[:], half(x_hi, n), half(x_lo, n), True, True).then_inc(pe_logit_rows, 1)

            def logit_transposes():
                pe.wait_ge(logit_rows_copied, 2)
                for t in range(NT):
                    ins = nc.tensor.transpose(ps_aux[0][:, t * E:(t + 1) * E], logit_rows[:, t * P:(t + 1) * P], par[0:E, IDENT:IDENT + E])
                ins.then_inc(pe_logits, 1)

            def gate_transposes():
                pe.wait_ge(combine_done, 1)
                for n in range(2):
                    for j in range(TH):
                        ins = nc.tensor.transpose(ps_aux[n][0:E, j * P:(j + 1) * P], combine[:, n * TH + j, :], ident)
                    ins.then_inc(pe_gates, 1)

            def second_biases():
                for n in range(2):
                    pe.wait_ge(gates_copied, n + 1)
                    nc.tensor.matmul(ps_aux[n][:], sub[0:E, EXP_B2:EXP_B2 + D], combine_rows[:, n * HALF:(n + 1) * HALF],
                                     start=True, stop=True).then_inc(pe_b2, 1)

            def layer1(i, k, first=False):
                kk = k % PASS
                s, n, c, q = kk // UNITS, kk // C % 2, kk % C, kk % 4
                u = PASS * i + k
                if kk % UNITS == 0:
                    pe.wait_ge(w_lo_done, 2 * i + k // UNITS + 1)
                if first and k == 4:
                    pe.wait_ge(x_lo_done, 2)
                if not (first and k < 4):
                    pe.wait_ge(act_done, u - 3)
                split_product(ps_hid[q][:], w1(w_hi[s], c), w1(w_lo[s], c), half(x_hi, n), half(x_lo, n), True, True).then_inc(layer1_done, 1)

            def layer2(i, k, first=False):
                s, n, c, q = k // UNITS, k // C % 2, k % C, k % 4
                pe.wait_ge(lo_done, PASS * i + k + 1)
                if c == 0 and not (first and k < UNITS):
                    pe.wait_ge(gated_done, 4 * i + k // C - 1)
                split_product(ps_out[n][:], w2(w_hi[s], c), w2(w_lo[s], c), hid_hi[q][:], hid_lo[q][:], c == 0, c == C - 1).then_inc(layer2_done, 1)

            def final(n):
                pe.wait_ge(rotation_done, 1)
                pe.wait_ge(acc_done, 15 + n)
                for j in range(TH):
                    b = (n * TH + j) // 2
                    ins = nc.tensor.matmul(ps_final[b][:, j % 2 * D:(j % 2 + 1) * D], acc[n][:, j * P:(j + 1) * P], rotation[:, b, :],
                                           start=True, stop=True)
                    if j % 2:
                        ins.then_inc(pe_final, 1)

            pe.wait_ge(par_in, 16)
            raw_transposes(0)
            pe.wait_ge(onehot_done, 1)
            pe.wait_ge(sub_in, 16)
            mlp(0, SE, sub[0:SUBJECTS, SUBJ:SUBJ + SE], onehot[:], 0)
            mlp(1, SH, sub[0:SE, HYP_W1:HYP_W1 + SH], emb[:], 1)
            raw_transposes(1)
            mlp(2, SH, sub[:, HYP_W2:HYP_W2 + SH], hyp1[:], 2)
            z_transposes(0)
            mlp(3, SH // 2, sub[:, STY_W1:STY_W1 + SH // 2], hyp[:], 3)
            mlp(4, P, sub[0:SH // 2, STY_W2:STY_W2 + D], sty1[:], 4)
            mlp(5, P, sub[0:SH // 2, STY_W2 + D:STY_W2 + 2 * D], sty1[:], 4)
            z_transposes(1)
            pe.wait_ge(router_done, 1)
            pe.wait_ge(mlp_copied, 6)
            logit_rows_of(0)
            layer1(0, 0, first=True)
            layer1(0, 1, first=True)
            for k in range(PASS):
                if k == 0:
                    layer1(0, 2, first=True)
                    logit_rows_of(1)
                    layer2(0, 0, first=True)
                    logit_transposes()
                    continue
                layer1(0, k + 2, first=True)
                if k == 1:
                    pe.wait_ge(h_done, 2)
                layer2(0, k, first=True)
                if k == 5:
                    gate_transposes()
                if k == 6:
                    second_biases()
            with pe.Fori(1, 3) as i:
                for k in range(PASS):
                    layer1(i, k + 2)
                    layer2(i, k)
            for k in range(PASS):
                if k + 2 < PASS:
                    layer1(3, k + 2)
                layer2(3, k)
                if k == PASS - 1:
                    final(0)
            final(1)


def _pack(inputs):
    import numpy as np

    f = {k: np.asarray(v) for k, v in inputs.items()}
    g = lambda name: f["L0_cond_" + name]
    params = np.zeros((P, NPAR), np.float32)
    params[:, IDENT:IDENT + P] = np.eye(P)
    for d in range(P):
        params[d, PARTNER + (d ^ 1)] = 1.0 if d % 2 else -1.0
    for col, name in ((LN_G, "ln_g"), (LN_B, "ln_b"), (HYP_B1, "hyp_b1"), (HYP_B2, "hyp_b2")):
        params[:, col] = g(name)
    params[:SH // 2, STY_B1] = g("sty_b1")
    params[:, STY_BG] = g("sty_b2")[:D]
    params[:, STY_BB] = g("sty_b2")[D:]
    for d in range(P):
        params[d, ANGLE:ANGLE + B] = f["condB_theta"] if d % 4 < 2 else f["condB_phi"]
    params[:, ROUTER:ROUTER + E] = g("router_w")
    params[:, EXPERT_NO:EXPERT_NO + E] = np.arange(E)
    subnet = np.zeros((P, NSUB), np.float32)
    subnet[:, HYP_W2:HYP_W2 + SH] = g("hyp_w2")
    subnet[:, STY_W1:STY_W1 + SH // 2] = g("sty_w1")
    subnet[:SE, HYP_W1:HYP_W1 + SH] = g("hyp_w1")
    subnet[:SH // 2, STY_W2:STY_W2 + 2 * D] = g("sty_w2")
    subnet[:SUBJECTS, SUBJ:SUBJ + SE] = g("subj_emb")
    subnet[:E, EXP_B2:EXP_B2 + D] = g("exp_b2")
    w1 = g("exp_w1")
    w2 = g("exp_w2").reshape(E, C, P, D).transpose(0, 2, 1, 3).reshape(E, P, C * D)
    experts = np.ascontiguousarray(np.concatenate([w1, w2], axis=2))
    exp_b1 = np.ascontiguousarray(g("exp_b1").reshape(E, C, P).transpose(0, 2, 1))
    return {"x": np.ascontiguousarray(f["x"]), "itok": np.ascontiguousarray(f["itok_B_6_14"]), "params": params,
            "subnet": subnet, "experts": experts, "exp_b1": exp_b1}


def kernel(**inputs):
    import numpy as np
    import concourse.bacc as bacc
    from concourse.bass_utils import run_bass_kernel_spmd

    nc = bacc.Bacc("TRN2", target_bir_lowering=False, num_devices=1)
    arrays, args = {}, {}
    for name, a in _pack(inputs).items():
        arrays["in_" + name] = a
        args[name] = nc.dram_tensor("in_" + name, a.shape, mybir.dt.from_np(a.dtype), kind="ExternalInput").ap()
    args["out"] = nc.dram_tensor("out_y", (B, T, D), mybir.dt.from_np(np.dtype("float32")), kind="ExternalOutput").ap()
    moe_rotate(nc, **args)
    r = run_bass_kernel_spmd(nc, [arrays], core_ids=[0])
    return r.results[0]["out_y"]
```

```python
from contextlib import ExitStack

import concourse.bass as bass
from concourse import mybir

ALU = mybir.AluOpType
ACT = mybir.ActivationFunctionType
F32 = mybir.dt.float32
F32R = mybir.dt.float32r
I32 = mybir.dt.int32
U32 = mybir.dt.uint32

P = 128
B = 4
T = 256
D = 128
E = 8
FF = 512
C = FF // P
NT = B * T // P
HALF = 512
TH = HALF // P
N = B * T
SUBJECTS, SE, SH = 32, 64, 128
UNITS = 2 * C
PASS = 2 * UNITS
AHEAD = 3
GATE_AT = 2
GATES_AT = 8
WCOLS = FF + C * D

IDENT, PARTNER = 0, 128
(LN_G, LN_B, HYP_B1, HYP_B2, STY_B1, STY_BG, STY_BB) = range(256, 263)
ANGLE = 263
ROUTER = ANGLE + B
EXPERT_NO = ROUTER + E
EXP_B2 = EXPERT_NO + E
NPAR = EXP_B2 + E
HYP_W2, STY_W1, HYP_W1, STY_W2, SUBJ = 0, 128, 192, 320, 576
NSUB = 640

LN_EPS, TIME_EPS, GAMMA_EPS = 1e-5, 1e-8, 1e-8
TWO_PI_HI = 6.28125
TWO_PI_LO = 0.0019353071795864769
ROUND = 12582912.0
PI_BELOW = 3.1415925
HALF_PI = 1.5707963267948966


def moe_rotate(nc, x, itok, params, subnet, experts, biases, out):
    with ExitStack() as ctx:
        def sb(name, shape, dt=F32):
            return ctx.enter_context(nc.sbuf_tensor(name, shape, dt))

        def sem(name):
            return ctx.enter_context(nc.semaphore(name))

        par = sb("par", [P, NPAR])
        sub = sb("sub", [P, NSUB])
        itok_i = sb("itok_i", [SUBJECTS, B], I32)
        itok_f = sb("itok_f", [SUBJECTS, B])
        row_no = sb("row_no", [SUBJECTS, 1])
        onehot = sb("onehot", [SUBJECTS, B])
        consts = sb("consts", [P, 4])
        eps_ln, eps_time, one, half_pi = (consts[:, i:i + 1] for i in range(4))
        x_tok = sb("x_tok", [P, NT, D])
        z_tok = sb("z_tok", [P, NT, D])
        out_tok = sb("out_tok", [P, NT, D])
        tok_part = sb("tok_part", [P, NT, 6])
        tok_stat = sb("tok_stat", [P, NT, 2])
        tok_ln = sb("tok_ln", [P, NT])
        tok_guess = sb("tok_guess", [P, NT])
        tok_tmp = sb("tok_tmp", [P, 2, NT])
        tok_rstd = sb("tok_rstd", [P, NT])
        h = sb("h", [P, N])
        feat_part = sb("feat_part", [P, B, 6])
        feat_stat = sb("feat_stat", [P, B, 2])
        feat_ln = sb("feat_ln", [P, B])
        feat_guess = sb("feat_guess", [P, B])
        feat_tmp = sb("feat_tmp", [P, 5, B])
        feat_shift = sb("feat_shift", [P, B])
        feat_scale = sb("feat_scale", [P, B])
        scaled = sb("scaled", [P, N])
        x_hi = sb("x_hi", [P, N], F32R)
        x_lo = sb("x_lo", [P, N], F32R)
        emb = sb("emb", [SE, B])
        hyp1 = sb("hyp1", [SH, B])
        hyp = sb("hyp", [SH, B])
        sty1 = sb("sty1", [SH // 2, B])
        gamma_raw = sb("gamma_raw", [P, B])
        beta = sb("beta", [P, B])
        sp_abs = sb("sp_abs", [P, B])
        sp_exp = sb("sp_exp", [P, B])
        sp_ln = sb("sp_ln", [P, B])
        sp_one = sb("sp_one", [P, B])
        sp_err = sb("sp_err", [P, B])
        sp_log1p = sb("sp_log1p", [P, B])
        gamma = sb("gamma", [P, B])
        router_hi = sb("router_hi", [P, E], F32R)
        router_lo = sb("router_lo", [P, E], F32R)
        logit_rows = sb("logit_rows", [E, N])
        logits = sb("logits", [P, NT, E])
        top = sb("top", [P, NT, 8])
        top_at = sb("top_at", [P, NT, 8], U32)
        top_at_f = sb("top_at_f", [P, NT, 2])
        gap = sb("gap", [P, NT])
        gap_exp = sb("gap_exp", [P, NT])
        gap_sum = sb("gap_sum", [P, NT])
        gates = sb("gates", [P, NT, 2])
        picked = sb("picked", [P, 2, NT, E])
        combine = sb("combine", [P, E, NT])
        combine_rows = sb("combine_rows", [E * NT, P])
        w_raw = [sb(f"w_raw{i}", [P, WCOLS]) for i in range(2)]
        w_hi = [sb(f"w_hi{i}", [P, WCOLS], F32R) for i in range(2)]
        w_lo = [sb(f"w_lo{i}", [P, WCOLS], F32R) for i in range(2)]
        bias = [sb(f"bias{i}", [P, C]) for i in range(2)]
        gate_all = [sb(f"gate_all{i}", [P, N]) for i in range(2)]
        hid = [sb(f"hid{i}", [P, HALF]) for i in range(4)]
        hid_hi = [sb(f"hid_hi{i}", [P, HALF], F32R) for i in range(4)]
        hid_lo = [sb(f"hid_lo{i}", [P, HALF], F32R) for i in range(4)]
        gated = [sb(f"gated{i}", [P, HALF]) for i in range(2)]
        held_out = [sb(f"held_out{i}", [P, HALF]) for i in range(2)]
        acc = [sb(f"acc{i}", [P, HALF]) for i in range(2)]
        angle = sb("angle", [P, 4, B])
        sin_a = sb("sin_a", [P, B])
        cos_a = sb("cos_a", [P, B])
        rot_tmp = sb("rot_tmp", [P, 2, B, D])
        rotation = sb("rotation", [P, B, D])

        ps_hid = [ctx.enter_context(nc.psum_tensor(f"ps_hid{i}", [P, HALF], F32)) for i in range(4)]
        ps_out = [ctx.enter_context(nc.psum_tensor(f"ps_out{i}", [P, HALF], F32)) for i in range(2)]
        ps_aux = [ctx.enter_context(nc.psum_tensor(f"ps_aux{i}", [P, HALF], F32)) for i in range(2)]

        ps_final = [ps_aux, ps_hid[:2]]

        ps_z = [*ps_out, *ps_hid[2:]]

        gate_dram = nc.dram_tensor("gate_dram", [E, N], F32, kind="Internal").ap()

        x_in = [sem(f"x_in{n}") for n in range(2)]
        par_in, sub_in, itok_in = sem("par_in"), sem("sub_in"), sem("itok_in")
        w_in = [sem(f"w_in{i}") for i in range(2)]
        bias_in = [sem(f"bias_in{i}") for i in range(2)]
        gate_in = [sem(f"gate_in{i}") for i in range(2)]
        gate_out = sem("gate_out")
        out_done = sem("out_done")
        pool_step = sem("pool_step")
        onehot_done, consts_done, angle_done, rotation_done = (
            sem("onehot_done"), sem("consts_done"), sem("angle_done"), sem("rotation_done"))
        w_hi0_done, w_hi1_done, w_lo_first = sem("w_hi0_done"), sem("w_hi1_done"), sem("w_lo_first")
        z_done, top_done, acc_by_pool = sem("z_done"), sem("top_done"), sem("acc_by_pool")
        pe_raw, pe_z, pe_mlp = sem("pe_raw"), sem("pe_z"), sem("pe_mlp")
        pe_logit_rows, pe_logits, pe_gates, pe_final = (
            sem("pe_logit_rows"), sem("pe_logits"), sem("pe_gates"), sem("pe_final"))
        layer1_done, layer2_done = sem("layer1_done"), sem("layer2_done")
        raw_copied, mlp_copied = sem("raw_copied"), sem("mlp_copied")
        act_step = sem("act_step")
        tok_guessed, feat_guessed, h_done, x_hi_done = (
            sem("tok_guessed"), sem("feat_guessed"), sem("h_done"), sem("x_hi_done"))
        softplus_parts, gap_exp_done = sem("softplus_parts"), sem("gap_exp_done")
        logit_rows_copied, gates_copied = sem("logit_rows_copied"), sem("gates_copied")
        w_hi_done, w_lo_done = sem("w_hi_done"), sem("w_lo_done")
        last_gated, held_done = sem("last_gated"), sem("held_done")
        act_done, hi_done, lo_done = sem("act_done"), sem("hi_done"), sem("lo_done")
        trig_done, out_copied = sem("trig_done"), sem("out_copied")
        dve_step = sem("dve_step")
        styled = sem("styled")
        tok_stats, feat_stats, scaled_done, x_lo_done = (
            sem("tok_stats"), sem("feat_stats"), sem("scaled_done"), sem("x_lo_done"))
        router_done, logits_copied, gap_done, combine_done = (
            sem("router_done"), sem("logits_copied"), sem("gap_done"), sem("combine_done"))
        gates_done = sem("gates_done")
        gated_done, acc_done = sem("gated_done"), sem("acc_done")

        out_view = out.rearrange("b (p j) d -> b p (j d)", p=P)
        ident = par[:, IDENT:IDENT + P]

        def w1(w, c):
            return w[:, c * P:(c + 1) * P]

        def w2(w, c):
            return w[:, FF + c * D:FF + (c + 1) * D]

        def half(a, n):
            return a[:, n * HALF:(n + 1) * HALF]

        block = ctx.enter_context(nc.Block())

        @block.sync
        def _(sp):
            for n in range(2):
                nc.sync.dma_start(x_tok[:, n * TH:(n + 1) * TH, :].rearrange("p (b j) d -> p b (j d)", b=2),
                                  x[2 * n:2 * n + 2].rearrange("b (p j) d -> p b (j d)", p=P)).then_inc(x_in[n], 16)
            nc.sync.dma_start(w_raw[0][:], experts[0]).then_inc(w_in[0], 16)
            nc.sync.dma_start(bias[0][:], biases[0]).then_inc(bias_in[0], 16)
            nc.sync.dma_start(bias[1][:], biases[1]).then_inc(bias_in[1], 16)
            nc.sync.dma_start(w_raw[1][:], experts[1]).then_inc(w_in[1], 16)
            for e in (0, 1):
                sp.wait_ge(w_lo_first, e + 1)
                nc.sync.dma_start(w_raw[e][:], experts[e + 2]).then_inc(w_in[e], 16)
            sp.wait_ge(gates_copied, 1)
            nc.sync.dma_start(gate_dram.rearrange("e (t p) -> (e t) p", p=P), combine_rows[:]).then_inc(gate_out, 16)
            sp.wait_ge(gate_out, 16)
            for e in (0, 1):
                nc.sync.dma_start(gate_all[e][:], gate_dram[e:e + 1, :].partition_broadcast(P)).then_inc(gate_in[e], 16)

            def prefetch(i, s, weights=True):
                e = 2 * i + s
                sp.wait_ge(act_done, UNITS * e)
                nc.sync.dma_start(bias[1 - s][:], biases[bass.ds(e + 1, 1)].rearrange("e p c -> (e p) c")).then_inc(bias_in[1 - s], 16)
                sp.wait_ge(gated_done, 2 * e)
                nc.sync.dma_start(gate_all[1 - s][:], gate_dram[bass.ds(e + 1, 1), :].partition_broadcast(P)).then_inc(gate_in[1 - s], 16)
                if weights:
                    sp.wait_ge(w_lo_done, e - 1)
                    nc.sync.dma_start(w_raw[s][:], experts[bass.ds(e + 2, 1)].rearrange("e p c -> (e p) c")).then_inc(w_in[s], 16)

            prefetch(0, 1, weights=False)
            with sp.Fori(1, 3) as i:
                prefetch(i, 0)
                prefetch(i, 1)
            prefetch(3, 0, weights=False)
            for b in (0, 1):
                sp.wait_ge(out_copied, b + 1)
                nc.sync.dma_start(out_view[b], out_tok[:, 2 * b:2 * b + 2, :].rearrange("p j d -> p (j d)")).then_inc(out_done, 16)
            sp.wait_ge(out_copied, 3)
            nc.sync.dma_start(out_view[2], out_tok[:, 4:6, :].rearrange("p j d -> p (j d)")).then_inc(out_done, 16)
            sp.wait_ge(out_done, 16 * B)

        @block.gpsimd
        def _(pool):
            steps = [0]

            def link(ins):
                steps[0] += 1
                ins.then_inc(pool_step, 1)
                pool.wait_ge(pool_step, steps[0])

            nc.gpsimd.dma_start(itok_i[:], itok.rearrange("(o b) -> o b", o=1).partition_broadcast(SUBJECTS)).then_inc(itok_in, 16)
            nc.gpsimd.memset(eps_ln, LN_EPS)
            nc.gpsimd.memset(eps_time, TIME_EPS)
            nc.gpsimd.memset(one, 1.0)
            nc.gpsimd.memset(half_pi, HALF_PI).then_inc(consts_done, 1)
            link(nc.gpsimd.iota(row_no[:], [[0, 1]], base=0, channel_multiplier=1, allow_small_or_imprecise_dtypes=True))
            pool.wait_ge(itok_in, 16)
            link(nc.gpsimd.tensor_copy(itok_f[:], itok_i[:]))
            nc.gpsimd.tensor_scalar(onehot[:], itok_f[:], row_no[:, 0:1], None, ALU.is_equal).then_inc(onehot_done, 1)
            pool.wait_ge(w_hi0_done, 1)
            nc.gpsimd.tensor_tensor(w_lo[0][:], w_raw[0][:], w_hi[0][:].bitcast(F32), ALU.subtract).then_inc(w_lo_first, 1)
            pool.wait_ge(w_in[1], 16)
            nc.gpsimd.tensor_copy(w_hi[1][:], w_raw[1][:]).then_inc(w_hi1_done, 1)
            pool.wait_ge(w_hi1_done, 1)
            nc.gpsimd.tensor_tensor(w_lo[1][:], w_raw[1][:], w_hi[1][:].bitcast(F32), ALU.subtract).then_inc(w_lo_first, 1)
            pool.wait_ge(par_in, 16)
            a = par[:, ANGLE:ANGLE + B]
            link(nc.gpsimd.tensor_scalar(angle[:, 0, :], a, 0.15915494309189535, ROUND, ALU.mult, ALU.add))
            link(nc.gpsimd.tensor_scalar(angle[:, 0, :], angle[:, 0, :], ROUND, None, ALU.subtract))
            link(nc.gpsimd.tensor_scalar(angle[:, 1, :], angle[:, 0, :], TWO_PI_HI, None, ALU.mult))
            link(nc.gpsimd.tensor_scalar(angle[:, 2, :], angle[:, 0, :], TWO_PI_LO, None, ALU.mult))
            link(nc.gpsimd.tensor_tensor(angle[:, 3, :], a, angle[:, 1, :], ALU.subtract))
            link(nc.gpsimd.tensor_tensor(angle[:, 1, :], angle[:, 3, :], angle[:, 2, :], ALU.subtract))
            nc.gpsimd.tensor_scalar(angle[:, 0, :], angle[:, 1, :], PI_BELOW, -PI_BELOW, ALU.min, ALU.max).then_inc(angle_done, 1)
            pool.wait_ge(top_done, 1)
            pool.wait_ge(gates_done, 1)
            for j in range(2):
                ins = nc.gpsimd.tensor_tensor(picked[:, j], picked[:, j], gates[:, :, j:j + 1].to_broadcast([P, NT, E]), ALU.mult)
            link(ins)
            nc.gpsimd.tensor_tensor(combine[:].rearrange("p e t -> p t e"), picked[:, 0], picked[:, 1], ALU.add).then_inc(combine_done, 1)
            for n in range(2):
                pool.wait_ge(raw_copied, n + 1)
                pool.wait_ge(gated_done, n + 1)
                nc.gpsimd.tensor_tensor(acc[n][:], acc[n][:], gated[n][:], ALU.add).then_inc(acc_by_pool, 1)
            pool.wait_ge(trig_done, 1)
            for b in range(B):
                nc.gpsimd.tensor_scalar(rot_tmp[:, 0, b, :], ident, cos_a[:, b:b + 1], None, ALU.mult)
                link(nc.gpsimd.tensor_scalar(rot_tmp[:, 1, b, :], par[:, PARTNER:PARTNER + D], sin_a[:, b:b + 1], None, ALU.mult))
            nc.gpsimd.tensor_tensor(rotation[:], rot_tmp[:, 0], rot_tmp[:, 1], ALU.add).then_inc(rotation_done, 1)

        @block.scalar
        def _(act):
            nc.scalar.dma_start(sub[:], subnet).then_inc(sub_in, 16)
            nc.scalar.dma_start(par[:], params).then_inc(par_in, 16)
            nc.scalar.preload_act_table_set("natural_log_exp_and_others")
            steps = [0]

            def link(ins):
                steps[0] += 1
                ins.then_inc(act_step, 1)
                act.wait_ge(act_step, steps[0])

            def guess(n, stat, eps, ln, first, width, ready, done):
                act.wait_ge(ready, n + 1)
                s = slice(n * width, (n + 1) * width)
                link(nc.scalar.activation(ln[:, s], stat[:, s, 1], ACT.Ln, bias=eps))
                nc.scalar.activation(first[:, s], ln[:, s], ACT.Exp, scale=-0.5).then_inc(done, 1)

            def mlp(k, dst, rows, func, col):
                act.wait_ge(pe_mlp, k + 1)
                src = ps_hid[k // 5][0:rows, 8 * k:8 * k + B]
                if col is None:
                    ins = nc.scalar.copy(dst[:], src)
                else:
                    ins = nc.scalar.activation(dst[:], src, func, bias=par[0:rows, col:col + 1])
                ins.then_inc(mlp_copied, 1)

            def affine(b):
                act.wait_ge(pe_z, b + 1)
                nc.scalar.activation(h[:, b * T:(b + 1) * T], ps_z[b][:, 0:T], ACT.Identity, bias=par[:, LN_B:LN_B + 1],
                                     scale=par[:, LN_G:LN_G + 1]).then_inc(h_done, 1)

            def high_x(b):
                act.wait_ge(styled, b // 2 + 1)
                s = slice(b * T, (b + 1) * T)
                nc.scalar.activation(x_hi[:, s], h[:, s], ACT.Identity, bias=feat_shift[:, b:b + 1],
                                     scale=feat_scale[:, b:b + 1]).then_inc(x_hi_done, 1)

            mlp(0, emb, SE, None, None)
            act.wait_ge(consts_done, 1)
            guess(0, tok_stat, eps_ln, tok_ln, tok_guess, TH, tok_stats, tok_guessed)
            act.wait_ge(par_in, 16)
            mlp(1, hyp1, SH, ACT.Relu, HYP_B1)
            mlp(2, hyp, SH, ACT.Identity, HYP_B2)
            affine(0)
            mlp(3, sty1, SH // 2, ACT.Relu, STY_B1)
            guess(1, tok_stat, eps_ln, tok_ln, tok_guess, TH, tok_stats, tok_guessed)
            affine(1)
            mlp(4, gamma_raw, P, ACT.Identity, STY_BG)
            link(nc.scalar.activation(sp_abs[:], ps_hid[0][:, 32:32 + B], ACT.Abs, bias=par[:, STY_BG:STY_BG + 1]))
            link(nc.scalar.activation(sp_exp[:], sp_abs[:], ACT.Exp, scale=-1.0))
            nc.scalar.activation(sp_ln[:], sp_exp[:], ACT.Ln, bias=one).then_inc(softplus_parts, 1)
            mlp(5, beta, P, ACT.Identity, STY_BB)
            guess(0, feat_stat, eps_time, feat_ln, feat_guess, 2, feat_stats, feat_guessed)
            affine(2)
            affine(3)
            high_x(0)
            high_x(1)
            guess(1, feat_stat, eps_time, feat_ln, feat_guess, 2, feat_stats, feat_guessed)

            def split_high(i, s):
                n = 1 - s
                act.wait_ge(w_in[n], 16 * (i + 1 + s))
                act.wait_ge(layer2_done, PASS * i + s * UNITS)
                nc.scalar.copy(w_hi[n][:], w_raw[n][:]).then_inc(w_hi_done, 1)

            def unit(i, k, first=False, split_next=True):
                s, q = k // UNITS, k % 4
                u = PASS * i + k
                if k % UNITS == 0:
                    act.wait_ge(bias_in[s], 16 * (i + 1))
                act.wait_ge(layer1_done, u + 1)
                b1 = bias[s][:, k % C:k % C + 1]
                if q != 3:
                    if not (first and k < 4):
                        act.wait_ge(layer2_done, u - 3)
                    nc.scalar.activation(hid_hi[q][:], ps_hid[q][:], ACT.Relu, bias=b1)
                if not (first and k < 4):
                    act.wait_ge(lo_done, u - 3)
                nc.scalar.activation(hid[q][:], ps_hid[q][:], ACT.Relu, bias=b1).then_inc(act_done, 1)
                if k % UNITS == 3 and split_next and not first:
                    split_high(i, s)

            for k in range(PASS):
                unit(0, k, first=True)
                if k == 0:
                    high_x(2)
                    high_x(3)
                if k in (1, 2):
                    act.wait_ge(pe_logit_rows, k)
                    nc.scalar.copy(half(logit_rows, k - 1), ps_aux[k - 1][0:E, :]).then_inc(logit_rows_copied, 1)
                if k in (7, 11):
                    n = k // 4 - 1
                    act.wait_ge(layer2_done, C * (n + 1))
                    nc.scalar.copy(held_out[n][:], ps_out[n][:]).then_inc(held_done, 1)
                if k == 10:
                    split_high(0, 1)
                if k == 5:
                    act.wait_ge(gap_done, 1)
                    nc.scalar.activation(gap_exp[:], gap[:], ACT.Exp).then_inc(gap_exp_done, 1)
                if k == GATES_AT:
                    act.wait_ge(pe_gates, 1)
                    nc.scalar.copy(combine_rows[:], ps_aux[1][0:E * NT, 0:P]).then_inc(gates_copied, 1)
                if k in (11, 12):
                    n = k - 11
                    act.wait_ge(pe_raw, n + 1)
                    nc.scalar.copy(acc[n][:], ps_aux[n][:]).then_inc(raw_copied, 1)
            with act.Fori(1, 3) as i:
                for k in range(PASS):
                    unit(i, k)
            for k in range(PASS):
                unit(3, k, split_next=k < UNITS)
                if k == 5:
                    nc.scalar.preload_act_table_set("trig_and_small")
                if k == 7:
                    act.wait_ge(angle_done, 1)
                    nc.scalar.activation(sin_a[:], angle[:, 0, :], ACT.Sin)
                    link(nc.scalar.activation(angle[:, 1, :], angle[:, 0, :], ACT.Abs))
                    nc.scalar.activation(cos_a[:], angle[:, 1, :], ACT.Sin, bias=half_pi, scale=-1.0).then_inc(trig_done, 1)
            for b in range(B):
                act.wait_ge(pe_final, b + 1)
                nc.scalar.copy(out_tok[:, 2 * b:2 * b + 2, :].rearrange("p j d -> p (j d)"),
                               ps_final[b // 2][b % 2][:, 0:2 * D]).then_inc(out_copied, 1)
            act.wait_ge(out_copied, 4)
            nc.scalar.dma_start(out_view[3], out_tok[:, 6:8, :].rearrange("p j d -> p (j d)")).then_inc(out_done, 16)

        @block.vector
        def _(dve):
            steps = [0]

            def link(ins):
                steps[0] += 1
                ins.then_inc(dve_step, 1)
                dve.wait_ge(dve_step, steps[0])

            def token_stats(*tiles):
                ins = None
                for t in tiles:
                    ins = nc.vector.bn_stats(tok_part[:, t, :], x_tok[:, t, :])
                return ins

            def join_token_stats(n):
                for t in range(n * TH, (n + 1) * TH):
                    ins = nc.vector.bn_aggr(tok_stat[:, t, :], tok_part[:, t, :])
                ins.then_inc(tok_stats, 1)

            def refine(n, stat, eps, first, tmp, width, guessed):
                s = slice(n * width, (n + 1) * width)
                dve.wait_ge(guessed, n + 1)
                link(nc.vector.scalar_tensor_tensor(tmp[:, 0, s], stat[:, s, 1], eps, first[:, s], ALU.add, ALU.mult))
                return nc.vector.scalar_tensor_tensor(tmp[:, 1, s], tmp[:, 0, s], -0.5, first[:, s], ALU.mult, ALU.mult)

            def token_rstd(n, meanwhile=()):
                s = slice(n * TH, (n + 1) * TH)
                dve.wait_ge(tok_guessed, n + 1)
                nc.vector.scalar_tensor_tensor(tok_tmp[:, 0, s], tok_stat[:, s, 1], eps_ln, tok_guess[:, s], ALU.add, ALU.mult).then_inc(dve_step, 1)
                token_stats(*meanwhile[:1])
                dve.wait_ge(dve_step, steps[0] + 1)
                nc.vector.scalar_tensor_tensor(tok_tmp[:, 1, s], tok_tmp[:, 0, s], -0.5, tok_guess[:, s], ALU.mult, ALU.mult).then_inc(dve_step, 1)
                token_stats(*meanwhile[1:])
                dve.wait_ge(dve_step, steps[0] + 2)
                steps[0] += 2
                link(nc.vector.scalar_tensor_tensor(tok_rstd[:, s], tok_tmp[:, 1, s], 1.5, tok_guess[:, s], ALU.add, ALU.mult))

            def normalise(b):
                for t in (2 * b, 2 * b + 1):
                    ins = nc.vector.tensor_scalar(z_tok[:, t, :], x_tok[:, t, :], tok_stat[:, t, 0:1], tok_rstd[:, t:t + 1],
                                                  ALU.subtract, ALU.mult)
                ins.then_inc(z_done, 1)

            def feature_stats(b):
                dve.wait_ge(h_done, b + 1)
                return nc.vector.bn_stats(feat_part[:, b, :], h[:, b * T:(b + 1) * T])

            def join_feature_stats(n):
                for b in (2 * n, 2 * n + 1):
                    ins = nc.vector.bn_aggr(feat_stat[:, b, :], feat_part[:, b, :])
                ins.then_inc(feat_stats, 1)

            def style(n):
                s = slice(2 * n, 2 * n + 2)
                dve.wait_ge(feat_guessed, n + 1)
                nc.vector.scalar_tensor_tensor(feat_tmp[:, 2, s], gamma[:, s], GAMMA_EPS, feat_guess[:, s], ALU.add, ALU.mult).then_inc(dve_step, 1)
                steps[0] += 1
                refined = refine(n, feat_stat, eps_time, feat_guess, feat_tmp, 2, feat_guessed)
                steps[0] += 1
                refined.then_inc(dve_step, 1)
                link(nc.vector.tensor_tensor(feat_tmp[:, 3, s], feat_stat[:, s, 0], feat_tmp[:, 2, s], ALU.mult))
                nc.vector.scalar_tensor_tensor(feat_tmp[:, 4, s], feat_tmp[:, 1, s], 1.5, feat_tmp[:, 3, s], ALU.add, ALU.mult)
                link(nc.vector.scalar_tensor_tensor(feat_scale[:, s], feat_tmp[:, 1, s], 1.5, feat_tmp[:, 2, s], ALU.add, ALU.mult))
                nc.vector.tensor_tensor(feat_shift[:, s], beta[:, s], feat_tmp[:, 4, s], ALU.subtract).then_inc(styled, 1)
                dve.wait_ge(styled, n + 1)
                for b in (2 * n, 2 * n + 1):
                    c = slice(b * T, (b + 1) * T)
                    nc.vector.tensor_scalar(scaled[:, c], h[:, c], feat_scale[:, b:b + 1], feat_shift[:, b:b + 1],
                                            ALU.mult, ALU.add).then_inc(scaled_done, 1)

            def low_x(n):
                for b in (2 * n, 2 * n + 1):
                    c = slice(b * T, (b + 1) * T)
                    dve.wait_ge(x_hi_done, b + 1)
                    dve.wait_ge(scaled_done, b + 1)
                    ins = nc.vector.tensor_tensor(x_lo[:, c], scaled[:, c], x_hi[:, c].bitcast(F32), ALU.subtract)
                ins.then_inc(x_lo_done, 1)

            dve.wait_ge(x_in[0], 16)
            link(token_stats(0, 1, 2, 3))
            join_token_stats(0)
            dve.wait_ge(x_in[1], 16)
            token_stats(4, 5)
            token_rstd(0, meanwhile=(6, 7))
            normalise(0)
            normalise(1)
            join_token_stats(1)
            dve.wait_ge(w_in[0], 16)
            nc.vector.tensor_copy(w_hi[0][:], w_raw[0][:]).then_inc(w_hi0_done, 1)
            feature_stats(0)
            token_rstd(1)
            link(feature_stats(1))
            join_feature_stats(0)
            normalise(2)
            normalise(3)
            dve.wait_ge(softplus_parts, 1)
            link(nc.vector.tensor_scalar(sp_one[:], sp_exp[:], 1.0, None, ALU.add))
            link(nc.vector.scalar_tensor_tensor(sp_err[:], sp_one[:], -1.0, sp_exp[:], ALU.add, ALU.subtract))
            link(nc.vector.tensor_tensor(sp_log1p[:], sp_ln[:], sp_err[:], ALU.subtract))
            link(nc.vector.scalar_tensor_tensor(gamma[:], gamma_raw[:], 0.0, sp_log1p[:], ALU.max, ALU.add))
            style(0)
            feature_stats(2)
            low_x(0)
            link(feature_stats(3))
            join_feature_stats(1)
            dve.wait_ge(par_in, 16)
            link(nc.vector.tensor_copy(router_hi[:], par[:, ROUTER:ROUTER + E]))
            nc.vector.tensor_tensor(router_lo[:], par[:, ROUTER:ROUTER + E], router_hi[:].bitcast(F32), ALU.subtract).then_inc(router_done, 1)
            style(1)
            low_x(1)

            def pick_experts():
                dve.wait_ge(pe_logits, 1)
                link(nc.vector.tensor_copy(logits[:].rearrange("p t e -> p (t e)"), ps_aux[0][:, 0:NT * E]))
                for t in range(NT):
                    ins = nc.vector.max(top[:, t, :], logits[:, t, :])
                link(ins)
                nc.vector.tensor_tensor(gap[:], top[:, :, 1], top[:, :, 0], ALU.subtract).then_inc(gap_done, 1)

            def place_experts():
                for t in range(NT):
                    ins = nc.vector.max_index(top_at[:, t, :], top[:, t, :], logits[:, t, :])
                link(ins)
                link(nc.vector.tensor_copy(top_at_f[:], top_at[:, :, 0:2]))
                numbers = par[:, EXPERT_NO:EXPERT_NO + E].unsqueeze(1).to_broadcast([P, NT, E])
                for j in range(2):
                    ins = nc.vector.tensor_tensor(picked[:, j], numbers, top_at_f[:, :, j:j + 1].to_broadcast([P, NT, E]), ALU.is_equal)
                ins.then_inc(top_done, 1)

            def top_gates():
                dve.wait_ge(gap_exp_done, 1)
                link(nc.vector.tensor_scalar(gap_sum[:], gap_exp[:], 1.0, None, ALU.add))
                link(nc.vector.reciprocal(gates[:, :, 0], gap_sum[:]))
                nc.vector.tensor_tensor(gates[:, :, 1], gap_exp[:], gates[:, :, 0], ALU.mult).then_inc(gates_done, 1)

            def gate_output(i, g, held=False):
                s, n = g // 2, g % 2
                if held:
                    dve.wait_ge(held_done, g + 1)
                else:
                    dve.wait_ge(layer2_done, PASS * i + C * (g + 1))
                if n == 0:
                    dve.wait_ge(gate_in[s], 16 * (i + 1))
                nc.vector.scalar_tensor_tensor(gated[n][:], held_out[n][:] if held else ps_out[n][:], par[:, bass.ds(EXP_B2 + 2 * i + s, 1)],
                                               half(gate_all[s], n), ALU.add, ALU.mult).then_inc(gated_done, 1)

            def add_output(i, g):
                n = g % 2
                dve.wait_ge(gated_done, 4 * i + g + 1)
                nc.vector.tensor_tensor(acc[n][:], acc[n][:], gated[n][:], ALU.add).then_inc(acc_done, 1)

            def split_low(i, s):
                n = 1 - s
                dve.wait_ge(w_hi_done, 2 * i + s)
                nc.vector.tensor_tensor(w_lo[n][:], w_raw[n][:], w_hi[n][:].bitcast(F32), ALU.subtract).then_inc(w_lo_done, 1)

            def unit(i, k, first=False, split_next=True):
                s, q = k // UNITS, k % 4
                u = PASS * i + k
                dve.wait_ge(act_done, u + 1)
                if not (first and k < 4):
                    dve.wait_ge(layer2_done, u - 3)
                if q == 3:
                    nc.vector.tensor_copy(hid_hi[q][:], hid[q][:]).then_inc(hi_done, 1)
                    dve.wait_ge(hi_done, 4 * i + k // 4 + 1)
                nc.vector.tensor_tensor(hid_lo[q][:], hid[q][:], hid_hi[q][:].bitcast(F32), ALU.subtract).then_inc(lo_done, 1)
                if k % UNITS == 4 and split_next and not first:
                    split_low(i, s)

            def group_end(i, k):
                i, g = (i, k // 4 - 1) if k >= 4 else (i - 1, 3)
                if k % 4 == GATE_AT:
                    gate_output(i, g)
                if k % 4 == 3:
                    add_output(i, g)

            for k in range(PASS):
                unit(0, k, first=True)
                if k == 3:
                    pick_experts()
                if k == 4:
                    place_experts()
                if k == 5:
                    top_gates()
                if k == 10:
                    split_low(0, 1)
                if k == 12:
                    gate_output(0, 0, held=True)
                if k == 13:
                    gate_output(0, 1, held=True)
                if k > 13:
                    if k % 4 == GATE_AT:
                        dve.wait_ge(acc_by_pool, 1)
                    group_end(0, k)
            dve.wait_ge(acc_by_pool, 2)
            with dve.Fori(1, 3) as i:
                for k in range(PASS):
                    unit(i, k)
                    group_end(i, k)
            for k in range(PASS):
                unit(3, k, split_next=k < UNITS)
                group_end(3, k)
            dve.wait_ge(layer2_done, 4 * PASS)
            for j in range(2):
                c = slice(j * T, (j + 1) * T)
                nc.vector.scalar_tensor_tensor(gated[1][:, c], ps_out[1][:, c], par[:, EXP_B2 + E - 1:EXP_B2 + E],
                                               gate_all[1][:, HALF + j * T:HALF + (j + 1) * T], ALU.add, ALU.mult).then_inc(last_gated, 1)

        @block.tensor
        def _(pe):
            def raw_transposes(n):
                pe.wait_ge(x_in[n], 16)
                for j in range(TH):
                    ins = nc.tensor.transpose(ps_aux[n][:, j * P:(j + 1) * P], x_tok[:, n * TH + j, :], ident)
                ins.then_inc(pe_raw, 1)

            def z_transposes(b):
                pe.wait_ge(z_done, b + 1)
                for j in range(2):
                    ins = nc.tensor.transpose(ps_z[b][:, j * P:(j + 1) * P], z_tok[:, 2 * b + j, :], ident)
                ins.then_inc(pe_z, 1)

            def keep_warm(count):
                for j in range(count):
                    nc.tensor.matmul(ps_aux[1][:], w1(w_hi[0], 0), w_hi[0][:, 0:HALF], start=True, stop=True)

            def mlp(k, rows, weight, moving, need):
                if need:
                    pe.wait_ge(mlp_copied, need)
                nc.tensor.matmul(ps_hid[k // 5][0:rows, 8 * k:8 * k + B], weight, moving, start=True, stop=True).then_inc(pe_mlp, 1)

            def split_product(out_, hi, lo, moving_hi, moving_lo, start, stop, half_ready=None):
                nc.tensor.matmul(out_, hi, moving_hi, start=start, stop=False)
                nc.tensor.matmul(out_, lo, moving_hi, start=False, stop=False)
                if half_ready:
                    pe.wait_ge(x_lo_done, half_ready)
                return nc.tensor.matmul(out_, hi, moving_lo, start=False, stop=stop)

            def logit_rows_of(n):
                pe.wait_ge(x_lo_done, n + 1)
                split_product(ps_aux[n][0:E, :], router_hi[:], router_lo[:], half(x_hi, n), half(x_lo, n), True, True).then_inc(pe_logit_rows, 1)

            def logit_transposes():
                pe.wait_ge(logit_rows_copied, 2)
                for t in range(NT):
                    ins = nc.tensor.transpose(ps_aux[0][:, t * E:(t + 1) * E], logit_rows[:, t * P:(t + 1) * P], par[0:E, IDENT:IDENT + E])
                ins.then_inc(pe_logits, 1)

            def gate_transposes():
                pe.wait_ge(combine_done, 1)
                nc.tensor.transpose(ps_aux[1][0:E * NT, 0:P], combine[:].rearrange("p e t -> p (e t)"), ident).then_inc(pe_gates, 1)

            def layer1(i, k, first=False):
                kk = k % PASS
                s, n, c, q = kk // UNITS, kk // C % 2, kk % C, kk % 4
                u = PASS * i + k
                if kk % UNITS == 0:
                    if first and k < PASS:
                        pe.wait_ge(w_lo_first, s + 1)
                    else:
                        pe.wait_ge(w_lo_done, 2 * i + k // UNITS - 1)
                if first and k in (0, 4):
                    pe.wait_ge(x_hi_done, k // 2 + 2)
                if not (first and k < 4):
                    pe.wait_ge(act_done, u - 3)
                split_product(ps_hid[q][:], w1(w_hi[s], c), w1(w_lo[s], c), half(x_hi, n), half(x_lo, n), True, True,
                              half_ready=n + 1 if first and k in (0, 4) else None).then_inc(layer1_done, 1)

            def layer2(i, k, first=False):
                s, n, c, q = k // UNITS, k // C % 2, k % C, k % 4
                pe.wait_ge(lo_done, PASS * i + k + 1)
                if c == 0 and first and k >= UNITS:
                    pe.wait_ge(held_done, k // C - 1)
                if c == 0 and not first:
                    pe.wait_ge(gated_done, 4 * i + k // C - 1)
                split_product(ps_out[n][:], w2(w_hi[s], c), w2(w_lo[s], c), hid_hi[q][:], hid_lo[q][:], c == 0, c == C - 1).then_inc(layer2_done, 1)

            def final(n, last):
                src = gated[1] if last else acc[n]
                if not last:
                    pe.wait_ge(rotation_done, 1)
                    pe.wait_ge(act_done, E * UNITS)
                    pe.wait_ge(acc_done, 13 - n)
                for j in range(TH):
                    b = (n * TH + j) // 2
                    if last and j % 2 == 0:
                        pe.wait_ge(last_gated, j // 2 + 1)
                    ins = nc.tensor.matmul(ps_final[n][j // 2][:, j % 2 * D:(j % 2 + 1) * D], src[:, j * P:(j + 1) * P],
                                           rotation[:, b, :], start=n == 0 or not last and j % 2 == 0,
                                           stop=last or n == 0, skip_group_check=n == 1)
                    if j % 2 and (last or n == 0):
                        ins.then_inc(pe_final, 1)

            pe.wait_ge(onehot_done, 1)
            pe.wait_ge(sub_in, 16)
            mlp(0, SE, sub[0:SUBJECTS, SUBJ:SUBJ + SE], onehot[:], 0)
            mlp(1, SH, sub[0:SE, HYP_W1:HYP_W1 + SH], emb[:], 1)
            mlp(2, SH, sub[:, HYP_W2:HYP_W2 + SH], hyp1[:], 2)
            pe.wait_ge(par_in, 16)
            z_transposes(0)
            mlp(3, SH // 2, sub[:, STY_W1:STY_W1 + SH // 2], hyp[:], 3)
            z_transposes(1)
            mlp(4, P, sub[0:SH // 2, STY_W2:STY_W2 + D], sty1[:], 4)
            mlp(5, P, sub[0:SH // 2, STY_W2 + D:STY_W2 + 2 * D], sty1[:], 4)
            pe.wait_ge(w_hi0_done, 1)
            z_transposes(2)
            keep_warm(2)
            z_transposes(3)
            keep_warm(4)
            pe.wait_ge(mlp_copied, 6)
            for k in range(AHEAD):
                if k == 2:
                    pe.wait_ge(h_done, B)
                layer1(0, k, first=True)
                if k == 0:
                    pe.wait_ge(router_done, 1)
                    logit_rows_of(0)
            for k in range(PASS):
                layer1(0, k + AHEAD, first=True)
                if k == 0:
                    logit_rows_of(1)
                layer2(0, k, first=True)
                if k == 2:
                    logit_transposes()
                if k == 6:
                    gate_transposes()
                if k == 9:
                    raw_transposes(0)
                    pe.wait_ge(gates_copied, 1)
                    raw_transposes(1)
            with pe.Fori(1, 3) as i:
                for k in range(PASS):
                    layer1(i, k + AHEAD)
                    layer2(i, k)
            for k in range(PASS):
                if k + AHEAD < PASS:
                    layer1(3, k + AHEAD)
                layer2(3, k)
                if k == PASS - 2:
                    final(1, False)
            final(0, False)
            final(1, True)


def _pack(inputs):
    import numpy as np

    f = {k: np.asarray(v) for k, v in inputs.items()}
    g = lambda name: f["L0_cond_" + name]
    params = np.zeros((P, NPAR), np.float32)
    params[:, IDENT:IDENT + P] = np.eye(P)
    for d in range(P):
        params[d, PARTNER + (d ^ 1)] = 1.0 if d % 2 else -1.0
    for col, name in ((LN_G, "ln_g"), (LN_B, "ln_b"), (HYP_B1, "hyp_b1"), (HYP_B2, "hyp_b2")):
        params[:, col] = g(name)
    params[:SH // 2, STY_B1] = g("sty_b1")
    params[:, STY_BG] = g("sty_b2")[:D]
    params[:, STY_BB] = g("sty_b2")[D:]
    for d in range(P):
        params[d, ANGLE:ANGLE + B] = f["condB_theta"] if d % 4 < 2 else f["condB_phi"]
    params[:, ROUTER:ROUTER + E] = g("router_w")
    params[:, EXP_B2:EXP_B2 + E] = g("exp_b2").T
    params[:, EXPERT_NO:EXPERT_NO + E] = np.arange(E)
    subnet = np.zeros((P, NSUB), np.float32)
    subnet[:, HYP_W2:HYP_W2 + SH] = g("hyp_w2")
    subnet[:, STY_W1:STY_W1 + SH // 2] = g("sty_w1")
    subnet[:SE, HYP_W1:HYP_W1 + SH] = g("hyp_w1")
    subnet[:SH // 2, STY_W2:STY_W2 + 2 * D] = g("sty_w2")
    subnet[:SUBJECTS, SUBJ:SUBJ + SE] = g("subj_emb")
    w1 = g("exp_w1")
    w2 = g("exp_w2").reshape(E, C, P, D).transpose(0, 2, 1, 3).reshape(E, P, C * D)
    experts = np.ascontiguousarray(np.concatenate([w1, w2], axis=2))
    biases = g("exp_b1").reshape(E, C, P).transpose(0, 2, 1)
    return {"x": np.ascontiguousarray(f["x"]), "itok": np.ascontiguousarray(f["itok_B_6_14"]), "params": params,
            "subnet": subnet, "experts": experts, "biases": np.ascontiguousarray(biases)}


def kernel(**inputs):
    import numpy as np
    import concourse.bacc as bacc
    from concourse.bass_utils import run_bass_kernel_spmd

    nc = bacc.Bacc("TRN2", target_bir_lowering=False, num_devices=1)
    arrays, args = {}, {}
    for name, a in _pack(inputs).items():
        arrays["in_" + name] = a
        args[name] = nc.dram_tensor("in_" + name, a.shape, mybir.dt.from_np(a.dtype), kind="ExternalInput").ap()
    args["out"] = nc.dram_tensor("out_y", (B, T, D), mybir.dt.from_np(np.dtype("float32")), kind="ExternalOutput").ap()
    moe_rotate(nc, **args)
    r = run_bass_kernel_spmd(nc, [arrays], core_ids=[0])
    return r.results[0]["out_y"]
```

```python
from contextlib import ExitStack

import concourse.bass as bass
from concourse import mybir

ALU = mybir.AluOpType
ACT = mybir.ActivationFunctionType
F32 = mybir.dt.float32
F32R = mybir.dt.float32r
I32 = mybir.dt.int32
U32 = mybir.dt.uint32

P = 128
B = 4
T = 256
D = 128
E = 8
FF = 512
C = FF // P
NT = B * T // P
HALF = 512
TH = HALF // P
N = B * T
SUBJECTS, SE, SH = 32, 64, 128
UNITS = 2 * C
PASS = 2 * UNITS
AHEAD = 3
GATE_AT = 2
GATES_AT = 7
WCOLS = FF + C * D

IDENT, PARTNER = 0, 128
(LN_G, LN_B, HYP_B1, HYP_B2, STY_B1, STY_BG, STY_BB) = range(256, 263)
ANGLE = 263
ROUTER = ANGLE + B
EXPERT_NO = ROUTER + E
EXP_B2 = EXPERT_NO + E
NPAR = EXP_B2 + E
HYP_W2, STY_W1, HYP_W1, STY_W2, SUBJ = 0, 128, 192, 320, 576
NSUB = 640

LN_EPS, TIME_EPS, GAMMA_EPS = 1e-5, 1e-8, 1e-8
TWO_PI_HI = 6.28125
TWO_PI_LO = 0.0019353071795864769
ROUND = 12582912.0
PI_BELOW = 3.1415925
HALF_PI = 1.5707963267948966


def moe_rotate(nc, x, itok, params, subnet, experts, biases, out):
    with ExitStack() as ctx:
        def sb(name, shape, dt=F32):
            return ctx.enter_context(nc.sbuf_tensor(name, shape, dt))

        def sem(name):
            return ctx.enter_context(nc.semaphore(name))

        par = sb("par", [P, NPAR])
        sub = sb("sub", [P, NSUB])
        itok_i = sb("itok_i", [SUBJECTS, B], I32)
        itok_f = sb("itok_f", [SUBJECTS, B])
        row_no = sb("row_no", [SUBJECTS, 1])
        onehot = sb("onehot", [SUBJECTS, B])
        consts = sb("consts", [P, 4])
        eps_ln, eps_time, one, half_pi = (consts[:, i:i + 1] for i in range(4))
        x_tok = sb("x_tok", [P, NT, D])
        z_tok = sb("z_tok", [P, NT, D])
        out_tok = sb("out_tok", [P, NT, D])
        tok_part = sb("tok_part", [P, NT, 6])
        tok_stat = sb("tok_stat", [P, NT, 2])
        tok_ln = sb("tok_ln", [P, NT])
        tok_guess = sb("tok_guess", [P, NT])
        tok_tmp = sb("tok_tmp", [P, 2, NT])
        tok_rstd = sb("tok_rstd", [P, NT])
        h = sb("h", [P, N])
        feat_part = sb("feat_part", [P, B, 6])
        feat_stat = sb("feat_stat", [P, B, 2])
        feat_ln = sb("feat_ln", [P, B])
        feat_guess = sb("feat_guess", [P, B])
        feat_tmp = sb("feat_tmp", [P, 5, B])
        feat_shift = sb("feat_shift", [P, B])
        feat_scale = sb("feat_scale", [P, B])
        scaled = sb("scaled", [P, N])
        x_hi = sb("x_hi", [P, N], F32R)
        x_lo = sb("x_lo", [P, N], F32R)
        emb = sb("emb", [SE, B])
        hyp1 = sb("hyp1", [SH, B])
        hyp = sb("hyp", [SH, B])
        sty1 = sb("sty1", [SH // 2, B])
        gamma_raw = sb("gamma_raw", [P, B])
        beta = sb("beta", [P, B])
        sp_abs = sb("sp_abs", [P, B])
        sp_exp = sb("sp_exp", [P, B])
        sp_ln = sb("sp_ln", [P, B])
        sp_one = sb("sp_one", [P, B])
        sp_err = sb("sp_err", [P, B])
        sp_log1p = sb("sp_log1p", [P, B])
        gamma = sb("gamma", [P, B])
        logits = sb("logits", [P, NT, E])
        top = sb("top", [P, NT, 8])
        top_at = sb("top_at", [P, NT, 8], U32)
        gap = sb("gap", [P, NT])
        gap_exp = sb("gap_exp", [P, NT])
        gap_sum = sb("gap_sum", [P, NT])
        gates = sb("gates", [P, NT, 2])
        picked = sb("picked", [P, 2, NT, E])
        combine = sb("combine", [P, E, NT])
        combine_rows = sb("combine_rows", [E * NT, P])
        w_raw = [sb(f"w_raw{i}", [P, WCOLS]) for i in range(2)]
        w_hi = [sb(f"w_hi{i}", [P, WCOLS], F32R) for i in range(2)]
        w_lo = [sb(f"w_lo{i}", [P, WCOLS], F32R) for i in range(2)]
        bias = [sb(f"bias{i}", [P, C]) for i in range(2)]
        gate_all = [sb(f"gate_all{i}", [P, N]) for i in range(2)]
        hid = [sb(f"hid{i}", [P, HALF]) for i in range(4)]
        hid_hi = [sb(f"hid_hi{i}", [P, HALF], F32R) for i in range(4)]
        hid_lo = [sb(f"hid_lo{i}", [P, HALF], F32R) for i in range(4)]
        gated = [sb(f"gated{i}", [P, HALF]) for i in range(2)]
        acc = [sb(f"acc{i}", [P, HALF]) for i in range(2)]
        angle = sb("angle", [P, 4, B])
        sin_a = sb("sin_a", [P, B])
        cos_a = sb("cos_a", [P, B])
        rot_tmp = sb("rot_tmp", [P, 2, B, D])
        rotation = sb("rotation", [P, B, D])

        ps_hid = [ctx.enter_context(nc.psum_tensor(f"ps_hid{i}", [P, HALF], F32)) for i in range(4)]
        ps_out = [ctx.enter_context(nc.psum_tensor(f"ps_out{i}", [P, HALF], F32)) for i in range(2)]
        ps_aux = [ctx.enter_context(nc.psum_tensor(f"ps_aux{i}", [P, HALF], F32)) for i in range(2)]

        ps_final = [ps_aux, ps_hid[:2]]

        first_banks = [ps_out[0], ps_aux[1], ps_aux[0], ps_out[1]]
        ps_z = [*ps_out, *ps_hid[2:]]

        gate_dram = nc.dram_tensor("gate_dram", [E, N], F32, kind="Internal").ap()

        x_in = [sem(f"x_in{n}") for n in range(2)]
        par_in, sub_in, itok_in = sem("par_in"), sem("sub_in"), sem("itok_in")
        w_in = [sem(f"w_in{i}") for i in range(2)]
        bias_in = [sem(f"bias_in{i}") for i in range(2)]
        gate_in = [sem(f"gate_in{i}") for i in range(2)]
        gate_out = sem("gate_out")
        out_done = sem("out_done")
        pool_step = sem("pool_step")
        onehot_done, consts_done, angle_done, rotation_done = (
            sem("onehot_done"), sem("consts_done"), sem("angle_done"), sem("rotation_done"))
        w_hi0_done, w_hi1_done, w_lo_first = sem("w_hi0_done"), sem("w_hi1_done"), sem("w_lo_first")
        z_done, z_by_pool, tok_refined = sem("z_done"), sem("z_by_pool"), sem("tok_refined")
        top_done, acc_by_pool = sem("top_done"), sem("acc_by_pool")
        pe_x, pe_z, pe_mlp = sem("pe_x"), sem("pe_z"), sem("pe_mlp")
        pe_logits, pe_gates, pe_final = sem("pe_logits"), sem("pe_gates"), sem("pe_final")
        layer1_done, layer2_done = sem("layer1_done"), sem("layer2_done")
        x_copied, mlp_copied = sem("x_copied"), sem("mlp_copied")
        act_step = sem("act_step")
        tok_guessed, feat_guessed, h_done, x_hi_done = (
            sem("tok_guessed"), sem("feat_guessed"), sem("h_done"), sem("x_hi_done"))
        softplus_parts, gap_sum_done = sem("softplus_parts"), sem("gap_sum_done")
        gates_copied = sem("gates_copied")
        w_hi_done, w_lo_done = sem("w_hi_done"), sem("w_lo_done")
        last_gated = sem("last_gated")
        act_done, hi_done, lo_done = sem("act_done"), sem("hi_done"), sem("lo_done")
        trig_done, out_copied = sem("trig_done"), sem("out_copied")
        dve_step = sem("dve_step")
        styled = sem("styled")
        tok_stats, feat_stats, scaled_done, x_lo_done = (
            sem("tok_stats"), sem("feat_stats"), sem("scaled_done"), sem("x_lo_done"))
        logits_copied, gap_done, gates_done, combine_done = (
            sem("logits_copied"), sem("gap_done"), sem("gates_done"), sem("combine_done"))
        gated_done, acc_done = sem("gated_done"), sem("acc_done")

        out_view = out.rearrange("b (p j) d -> b p (j d)", p=P)
        ident = par[:, IDENT:IDENT + P]

        def w1(w, c):
            return w[:, c * P:(c + 1) * P]

        def w2(w, c):
            return w[:, FF + c * D:FF + (c + 1) * D]

        def half(a, n):
            return a[:, n * HALF:(n + 1) * HALF]

        block = ctx.enter_context(nc.Block())

        @block.sync
        def _(sp):
            for n in range(2):
                nc.sync.dma_start(x_tok[:, n * TH:(n + 1) * TH, :].rearrange("p (b j) d -> p b (j d)", b=2),
                                  x[2 * n:2 * n + 2].rearrange("b (p j) d -> p b (j d)", p=P)).then_inc(x_in[n], 16)
            nc.sync.dma_start(w_raw[0][:], experts[0]).then_inc(w_in[0], 16)
            nc.sync.dma_start(bias[0][:], biases[0]).then_inc(bias_in[0], 16)
            nc.sync.dma_start(bias[1][:], biases[1]).then_inc(bias_in[1], 16)
            nc.sync.dma_start(w_raw[1][:], experts[1]).then_inc(w_in[1], 16)
            for e in (0, 1):
                sp.wait_ge(w_lo_first, e + 1)
                nc.sync.dma_start(w_raw[e][:], experts[e + 2]).then_inc(w_in[e], 16)
            sp.wait_ge(gates_copied, 1)
            nc.sync.dma_start(gate_dram.rearrange("e (t p) -> (e t) p", p=P), combine_rows[:]).then_inc(gate_out, 16)
            sp.wait_ge(gate_out, 16)
            for e in (0, 1):
                nc.sync.dma_start(gate_all[e][:], gate_dram[e:e + 1, :].partition_broadcast(P)).then_inc(gate_in[e], 16)

            def prefetch(i, s, weights=True):
                e = 2 * i + s
                sp.wait_ge(act_done, UNITS * e)
                nc.sync.dma_start(bias[1 - s][:], biases[bass.ds(e + 1, 1)].rearrange("e p c -> (e p) c")).then_inc(bias_in[1 - s], 16)
                sp.wait_ge(gated_done, 2 * e)
                nc.sync.dma_start(gate_all[1 - s][:], gate_dram[bass.ds(e + 1, 1), :].partition_broadcast(P)).then_inc(gate_in[1 - s], 16)
                if weights:
                    sp.wait_ge(w_lo_done, e - 1)
                    nc.sync.dma_start(w_raw[s][:], experts[bass.ds(e + 2, 1)].rearrange("e p c -> (e p) c")).then_inc(w_in[s], 16)

            prefetch(0, 1, weights=False)
            with sp.Fori(1, 3) as i:
                prefetch(i, 0)
                prefetch(i, 1)
            prefetch(3, 0, weights=False)
            for b in (0, 1):
                sp.wait_ge(out_copied, b + 1)
                nc.sync.dma_start(out_view[b], out_tok[:, 2 * b:2 * b + 2, :].rearrange("p j d -> p (j d)")).then_inc(out_done, 16)
            sp.wait_ge(out_copied, 3)
            nc.sync.dma_start(out_view[2], out_tok[:, 4:6, :].rearrange("p j d -> p (j d)")).then_inc(out_done, 16)
            sp.wait_ge(out_done, 16 * B)

        @block.gpsimd
        def _(pool):
            steps = [0]

            def link(ins):
                steps[0] += 1
                ins.then_inc(pool_step, 1)
                pool.wait_ge(pool_step, steps[0])

            nc.gpsimd.dma_start(itok_i[:], itok.rearrange("(o b) -> o b", o=1).partition_broadcast(SUBJECTS)).then_inc(itok_in, 16)
            nc.gpsimd.memset(eps_ln, LN_EPS)
            nc.gpsimd.memset(eps_time, TIME_EPS)
            nc.gpsimd.memset(one, 1.0)
            nc.gpsimd.memset(half_pi, HALF_PI).then_inc(consts_done, 1)
            link(nc.gpsimd.iota(row_no[:], [[0, 1]], base=0, channel_multiplier=1, allow_small_or_imprecise_dtypes=True))
            pool.wait_ge(itok_in, 16)
            link(nc.gpsimd.tensor_copy(itok_f[:], itok_i[:]))
            nc.gpsimd.tensor_scalar(onehot[:], itok_f[:], row_no[:, 0:1], None, ALU.is_equal).then_inc(onehot_done, 1)
            pool.wait_ge(w_hi0_done, 1)
            nc.gpsimd.tensor_tensor(w_lo[0][:], w_raw[0][:], w_hi[0][:].bitcast(F32), ALU.subtract).then_inc(w_lo_first, 1)
            pool.wait_ge(tok_refined, 1)
            for t in (6, 7):
                ins = nc.gpsimd.tensor_scalar(z_tok[:, t, :], x_tok[:, t, :], tok_stat[:, t, 0:1], tok_rstd[:, t:t + 1],
                                              ALU.subtract, ALU.mult)
            ins.then_inc(z_by_pool, 1)
            pool.wait_ge(w_in[1], 16)
            nc.gpsimd.tensor_copy(w_hi[1][:], w_raw[1][:]).then_inc(w_hi1_done, 1)
            pool.wait_ge(w_hi1_done, 1)
            nc.gpsimd.tensor_tensor(w_lo[1][:], w_raw[1][:], w_hi[1][:].bitcast(F32), ALU.subtract).then_inc(w_lo_first, 1)
            pool.wait_ge(par_in, 16)
            a = par[:, ANGLE:ANGLE + B]
            link(nc.gpsimd.tensor_scalar(angle[:, 0, :], a, 0.15915494309189535, ROUND, ALU.mult, ALU.add))
            link(nc.gpsimd.tensor_scalar(angle[:, 0, :], angle[:, 0, :], ROUND, None, ALU.subtract))
            link(nc.gpsimd.tensor_scalar(angle[:, 1, :], angle[:, 0, :], TWO_PI_HI, None, ALU.mult))
            link(nc.gpsimd.tensor_scalar(angle[:, 2, :], angle[:, 0, :], TWO_PI_LO, None, ALU.mult))
            link(nc.gpsimd.tensor_tensor(angle[:, 3, :], a, angle[:, 1, :], ALU.subtract))
            link(nc.gpsimd.tensor_tensor(angle[:, 1, :], angle[:, 3, :], angle[:, 2, :], ALU.subtract))
            nc.gpsimd.tensor_scalar(angle[:, 0, :], angle[:, 1, :], PI_BELOW, -PI_BELOW, ALU.min, ALU.max).then_inc(angle_done, 1)
            pool.wait_ge(gates_done, 1)
            link(nc.gpsimd.tensor_tensor(gates[:, :, 1], gap_exp[:], gates[:, :, 0], ALU.mult))
            pool.wait_ge(top_done, 1)
            for j in range(2):
                ins = nc.gpsimd.tensor_tensor(picked[:, j], picked[:, j], gates[:, :, j:j + 1].to_broadcast([P, NT, E]), ALU.mult)
            link(ins)
            nc.gpsimd.tensor_tensor(combine[:].rearrange("p e t -> p t e"), picked[:, 0], picked[:, 1], ALU.add).then_inc(combine_done, 1)
            for n in range(2):
                pool.wait_ge(x_copied, n + 1)
                pool.wait_ge(gated_done, n + 1)
                nc.gpsimd.tensor_tensor(acc[n][:], acc[n][:], gated[n][:], ALU.add).then_inc(acc_by_pool, 1)
            pool.wait_ge(trig_done, 1)
            for b in range(B):
                nc.gpsimd.tensor_scalar(rot_tmp[:, 0, b, :], ident, cos_a[:, b:b + 1], None, ALU.mult)
                link(nc.gpsimd.tensor_scalar(rot_tmp[:, 1, b, :], par[:, PARTNER:PARTNER + D], sin_a[:, b:b + 1], None, ALU.mult))
            nc.gpsimd.tensor_tensor(rotation[:], rot_tmp[:, 0], rot_tmp[:, 1], ALU.add).then_inc(rotation_done, 1)

        @block.scalar
        def _(act):
            nc.scalar.dma_start(sub[:], subnet).then_inc(sub_in, 16)
            nc.scalar.dma_start(par[:], params).then_inc(par_in, 16)
            nc.scalar.preload_act_table_set("natural_log_exp_and_others")
            steps = [0]

            def link(ins):
                steps[0] += 1
                ins.then_inc(act_step, 1)
                act.wait_ge(act_step, steps[0])

            def guess(n, stat, eps, ln, first, width, ready, done):
                act.wait_ge(ready, n + 1)
                s = slice(n * width, (n + 1) * width)
                link(nc.scalar.activation(ln[:, s], stat[:, s, 1], ACT.Ln, bias=eps))
                nc.scalar.activation(first[:, s], ln[:, s], ACT.Exp, scale=-0.5).then_inc(done, 1)

            def mlp(k, dst, rows, func, col):
                act.wait_ge(pe_mlp, k + 1)
                src = ps_hid[k // 5][0:rows, 8 * k:8 * k + B]
                if col is None:
                    ins = nc.scalar.copy(dst[:], src)
                else:
                    ins = nc.scalar.activation(dst[:], src, func, bias=par[0:rows, col:col + 1])
                ins.then_inc(mlp_copied, 1)

            def affine(b):
                act.wait_ge(pe_z, b + 1)
                nc.scalar.activation(h[:, b * T:(b + 1) * T], ps_z[b][:, 0:T], ACT.Identity, bias=par[:, LN_B:LN_B + 1],
                                     scale=par[:, LN_G:LN_G + 1]).then_inc(h_done, 1)

            def copy_x(n):
                act.wait_ge(pe_x, n + 1)
                nc.scalar.copy(acc[n][:], ps_aux[n][:]).then_inc(x_copied, 1)

            def high_x(b):
                act.wait_ge(styled, b // 2 + 1)
                s = slice(b * T, (b + 1) * T)
                nc.scalar.activation(x_hi[:, s], h[:, s], ACT.Identity, bias=feat_shift[:, b:b + 1],
                                     scale=feat_scale[:, b:b + 1]).then_inc(x_hi_done, 1)

            mlp(0, emb, SE, None, None)
            act.wait_ge(consts_done, 1)
            guess(0, tok_stat, eps_ln, tok_ln, tok_guess, TH, tok_stats, tok_guessed)
            act.wait_ge(par_in, 16)
            mlp(1, hyp1, SH, ACT.Relu, HYP_B1)
            mlp(2, hyp, SH, ACT.Identity, HYP_B2)
            affine(0)
            mlp(3, sty1, SH // 2, ACT.Relu, STY_B1)
            guess(1, tok_stat, eps_ln, tok_ln, tok_guess, TH, tok_stats, tok_guessed)
            affine(1)
            mlp(4, gamma_raw, P, ACT.Identity, STY_BG)
            link(nc.scalar.activation(sp_abs[:], ps_hid[0][:, 32:32 + B], ACT.Abs, bias=par[:, STY_BG:STY_BG + 1]))
            link(nc.scalar.activation(sp_exp[:], sp_abs[:], ACT.Exp, scale=-1.0))
            nc.scalar.activation(sp_ln[:], sp_exp[:], ACT.Ln, bias=one).then_inc(softplus_parts, 1)
            mlp(5, beta, P, ACT.Identity, STY_BB)
            guess(0, feat_stat, eps_time, feat_ln, feat_guess, 2, feat_stats, feat_guessed)
            copy_x(0)
            copy_x(1)
            affine(2)
            high_x(0)
            high_x(1)
            affine(3)
            guess(1, feat_stat, eps_time, feat_ln, feat_guess, 2, feat_stats, feat_guessed)

            def split_high(i, s):
                n = 1 - s
                act.wait_ge(w_in[n], 16 * (i + 1 + s))
                act.wait_ge(layer2_done, PASS * i + s * UNITS)
                nc.scalar.copy(w_hi[n][:], w_raw[n][:]).then_inc(w_hi_done, 1)

            def unit(i, k, first=False, split_next=True):
                s, q = k // UNITS, k % 4
                u = PASS * i + k
                if k % UNITS == 0:
                    act.wait_ge(bias_in[s], 16 * (i + 1))
                act.wait_ge(layer1_done, u + 1)
                b1 = bias[s][:, k % C:k % C + 1]
                if q != 3:
                    if not (first and k < 4):
                        act.wait_ge(layer2_done, u - 3)
                    nc.scalar.activation(hid_hi[q][:], ps_hid[q][:], ACT.Relu, bias=b1)
                if not (first and k < 4):
                    act.wait_ge(lo_done, u - 3)
                nc.scalar.activation(hid[q][:], ps_hid[q][:], ACT.Relu, bias=b1).then_inc(act_done, 1)
                if k % UNITS == 3 and split_next and not first:
                    split_high(i, s)

            for k in range(PASS):
                unit(0, k, first=True)
                if k == 0:
                    high_x(2)
                    high_x(3)
                if k == 10:
                    split_high(0, 1)
                if k == 3:
                    act.wait_ge(gap_done, 1)
                    link(nc.scalar.activation(gap_exp[:], gap[:], ACT.Exp))
                    nc.scalar.activation(gap_sum[:], gap_exp[:], ACT.Identity, bias=one).then_inc(gap_sum_done, 1)
                if k == GATES_AT:
                    act.wait_ge(pe_gates, 1)
                    nc.scalar.copy(combine_rows[:], ps_aux[0][0:E * NT, 0:P]).then_inc(gates_copied, 1)
            with act.Fori(1, 3) as i:
                for k in range(PASS):
                    unit(i, k)
            for k in range(PASS):
                unit(3, k, split_next=k < UNITS)
                if k == 5:
                    nc.scalar.preload_act_table_set("trig_and_small")
                if k == 7:
                    act.wait_ge(angle_done, 1)
                    nc.scalar.activation(sin_a[:], angle[:, 0, :], ACT.Sin)
                    link(nc.scalar.activation(angle[:, 1, :], angle[:, 0, :], ACT.Abs))
                    nc.scalar.activation(cos_a[:], angle[:, 1, :], ACT.Sin, bias=half_pi, scale=-1.0).then_inc(trig_done, 1)
            for b in range(B):
                act.wait_ge(pe_final, b + 1)
                nc.scalar.copy(out_tok[:, 2 * b:2 * b + 2, :].rearrange("p j d -> p (j d)"),
                               ps_final[b // 2][b % 2][:, 0:2 * D]).then_inc(out_copied, 1)
            act.wait_ge(out_copied, B)
            nc.scalar.dma_start(out_view[3], out_tok[:, 6:8, :].rearrange("p j d -> p (j d)")).then_inc(out_done, 16)

        @block.vector
        def _(dve):
            steps = [0]

            def mark(ins):
                steps[0] += 1
                ins.then_inc(dve_step, 1)

            def marked():
                dve.wait_ge(dve_step, steps[0])

            def link(ins):
                mark(ins)
                marked()

            def token_stats(*tiles):
                ins = None
                for t in tiles:
                    ins = nc.vector.bn_stats(tok_part[:, t, :], x_tok[:, t, :])
                return ins

            def join_token_stats(n):
                for t in range(n * TH, (n + 1) * TH):
                    ins = nc.vector.bn_aggr(tok_stat[:, t, :], tok_part[:, t, :])
                ins.then_inc(tok_stats, 1)

            def refine(n, stat, eps, first, tmp, width, guessed):
                s = slice(n * width, (n + 1) * width)
                dve.wait_ge(guessed, n + 1)
                link(nc.vector.scalar_tensor_tensor(tmp[:, 0, s], stat[:, s, 1], eps, first[:, s], ALU.add, ALU.mult))
                return nc.vector.scalar_tensor_tensor(tmp[:, 1, s], tmp[:, 0, s], -0.5, first[:, s], ALU.mult, ALU.mult)

            def token_rstd(n, meanwhile=()):
                s = slice(n * TH, (n + 1) * TH)
                dve.wait_ge(tok_guessed, n + 1)
                nc.vector.scalar_tensor_tensor(tok_tmp[:, 0, s], tok_stat[:, s, 1], eps_ln, tok_guess[:, s], ALU.add, ALU.mult).then_inc(dve_step, 1)
                token_stats(*meanwhile[:1])
                dve.wait_ge(dve_step, steps[0] + 1)
                nc.vector.scalar_tensor_tensor(tok_tmp[:, 1, s], tok_tmp[:, 0, s], -0.5, tok_guess[:, s], ALU.mult, ALU.mult).then_inc(dve_step, 1)
                token_stats(*meanwhile[1:])
                dve.wait_ge(dve_step, steps[0] + 2)
                steps[0] += 2
                mark(nc.vector.scalar_tensor_tensor(tok_rstd[:, s], tok_tmp[:, 1, s], 1.5, tok_guess[:, s], ALU.add, ALU.mult))

            def normalise(*tiles):
                for t in tiles:
                    ins = nc.vector.tensor_scalar(z_tok[:, t, :], x_tok[:, t, :], tok_stat[:, t, 0:1], tok_rstd[:, t:t + 1],
                                                  ALU.subtract, ALU.mult)
                    if t % 2:
                        ins.then_inc(z_done, 1)
                return ins

            def feature_stats(b):
                dve.wait_ge(h_done, b + 1)
                return nc.vector.bn_stats(feat_part[:, b, :], h[:, b * T:(b + 1) * T])

            def join_feature_stats(n):
                for b in (2 * n, 2 * n + 1):
                    ins = nc.vector.bn_aggr(feat_stat[:, b, :], feat_part[:, b, :])
                ins.then_inc(feat_stats, 1)

            def style(n):
                s = slice(2 * n, 2 * n + 2)
                dve.wait_ge(feat_guessed, n + 1)
                nc.vector.scalar_tensor_tensor(feat_tmp[:, 2, s], gamma[:, s], GAMMA_EPS, feat_guess[:, s], ALU.add, ALU.mult).then_inc(dve_step, 1)
                steps[0] += 1
                refined = refine(n, feat_stat, eps_time, feat_guess, feat_tmp, 2, feat_guessed)
                steps[0] += 1
                refined.then_inc(dve_step, 1)
                link(nc.vector.tensor_tensor(feat_tmp[:, 3, s], feat_stat[:, s, 0], feat_tmp[:, 2, s], ALU.mult))
                nc.vector.scalar_tensor_tensor(feat_tmp[:, 4, s], feat_tmp[:, 1, s], 1.5, feat_tmp[:, 3, s], ALU.add, ALU.mult)
                link(nc.vector.scalar_tensor_tensor(feat_scale[:, s], feat_tmp[:, 1, s], 1.5, feat_tmp[:, 2, s], ALU.add, ALU.mult))
                nc.vector.tensor_tensor(feat_shift[:, s], beta[:, s], feat_tmp[:, 4, s], ALU.subtract).then_inc(styled, 1)
                dve.wait_ge(styled, n + 1)
                for b in (2 * n, 2 * n + 1):
                    c = slice(b * T, (b + 1) * T)
                    nc.vector.tensor_scalar(scaled[:, c], h[:, c], feat_scale[:, b:b + 1], feat_shift[:, b:b + 1],
                                            ALU.mult, ALU.add).then_inc(scaled_done, 1)

            def low_x(n):
                for b in (2 * n, 2 * n + 1):
                    c = slice(b * T, (b + 1) * T)
                    dve.wait_ge(x_hi_done, b + 1)
                    dve.wait_ge(scaled_done, b + 1)
                    ins = nc.vector.tensor_tensor(x_lo[:, c], scaled[:, c], x_hi[:, c].bitcast(F32), ALU.subtract)
                ins.then_inc(x_lo_done, 1)

            dve.wait_ge(x_in[0], 16)
            link(token_stats(0, 1, 2, 3))
            join_token_stats(0)
            dve.wait_ge(x_in[1], 16)
            token_stats(4, 5)
            token_rstd(0, meanwhile=(6, 7))
            marked()
            normalise(0, 1, 2, 3)
            join_token_stats(1)
            dve.wait_ge(w_in[0], 16)
            nc.vector.tensor_copy(w_hi[0][:], w_raw[0][:]).then_inc(w_hi0_done, 1)
            feature_stats(0)
            token_rstd(1)
            feature_stats(1).then_inc(tok_refined, 1)
            dve.wait_ge(tok_refined, 1)
            join_feature_stats(0)
            dve.wait_ge(softplus_parts, 1)
            mark(nc.vector.tensor_scalar(sp_one[:], sp_exp[:], 1.0, None, ALU.add))
            normalise(4)
            marked()
            mark(nc.vector.scalar_tensor_tensor(sp_err[:], sp_one[:], -1.0, sp_exp[:], ALU.add, ALU.subtract))
            normalise(5)
            marked()
            link(nc.vector.tensor_tensor(sp_log1p[:], sp_ln[:], sp_err[:], ALU.subtract))
            link(nc.vector.scalar_tensor_tensor(gamma[:], gamma_raw[:], 0.0, sp_log1p[:], ALU.max, ALU.add))
            style(0)
            feature_stats(2)
            low_x(0)
            link(feature_stats(3))
            join_feature_stats(1)
            style(1)

            def pick_experts():
                dve.wait_ge(pe_logits, 2)
                nc.vector.tensor_copy(logits[:].rearrange("p t e -> p (t e)"), ps_out[1][:, 0:NT * E]).then_inc(logits_copied, 1)
                dve.wait_ge(logits_copied, 1)
                for t in range(NT):
                    ins = nc.vector.max(top[:, t, :], logits[:, t, :])
                link(ins)
                nc.vector.tensor_tensor(gap[:], top[:, :, 1], top[:, :, 0], ALU.subtract).then_inc(gap_done, 1)

            def place_experts():
                for t in range(NT):
                    ins = nc.vector.max_index(top_at[:, t, :], top[:, t, :], logits[:, t, :])
                link(ins)
                numbers = par[:, EXPERT_NO:EXPERT_NO + E].unsqueeze(1).to_broadcast([P, NT, E])
                for j in range(2):
                    ins = nc.vector.tensor_tensor(picked[:, j], numbers, top_at[:, :, j:j + 1].to_broadcast([P, NT, E]), ALU.is_equal)
                ins.then_inc(top_done, 1)

            def top_gate():
                dve.wait_ge(gap_sum_done, 1)
                nc.vector.reciprocal(gates[:, :, 0], gap_sum[:]).then_inc(gates_done, 1)

            def gate_output(i, g, bank=None):
                s, n = g // 2, g % 2
                dve.wait_ge(layer2_done, PASS * i + C * (g + 1))
                if n == 0:
                    dve.wait_ge(gate_in[s], 16 * (i + 1))
                nc.vector.scalar_tensor_tensor(gated[n][:], (ps_out[n] if bank is None else bank)[:], par[:, bass.ds(EXP_B2 + 2 * i + s, 1)],
                                               half(gate_all[s], n), ALU.add, ALU.mult).then_inc(gated_done, 1)

            def add_output(i, g):
                n = g % 2
                dve.wait_ge(gated_done, 4 * i + g + 1)
                nc.vector.tensor_tensor(acc[n][:], acc[n][:], gated[n][:], ALU.add).then_inc(acc_done, 1)

            def split_low(i, s):
                n = 1 - s
                dve.wait_ge(w_hi_done, 2 * i + s)
                nc.vector.tensor_tensor(w_lo[n][:], w_raw[n][:], w_hi[n][:].bitcast(F32), ALU.subtract).then_inc(w_lo_done, 1)

            def unit(i, k, first=False, split_next=True):
                s, q = k // UNITS, k % 4
                u = PASS * i + k
                dve.wait_ge(act_done, u + 1)
                if not (first and k < 4):
                    dve.wait_ge(layer2_done, u - 3)
                if q == 3:
                    nc.vector.tensor_copy(hid_hi[q][:], hid[q][:]).then_inc(hi_done, 1)
                    dve.wait_ge(hi_done, 4 * i + k // 4 + 1)
                nc.vector.tensor_tensor(hid_lo[q][:], hid[q][:], hid_hi[q][:].bitcast(F32), ALU.subtract).then_inc(lo_done, 1)
                if k % UNITS == 4 and split_next and not first:
                    split_low(i, s)

            def group_end(i, k):
                i, g = (i, k // 4 - 1) if k >= 4 else (i - 1, 3)
                if k % 4 == GATE_AT:
                    gate_output(i, g)
                if k % 4 == 3:
                    add_output(i, g)

            for k in range(PASS):
                unit(0, k, first=True)
                if k == 0:
                    low_x(1)
                if k == 1:
                    pick_experts()
                if k == 3:
                    place_experts()
                if k == 4:
                    top_gate()
                if k == 10:
                    split_low(0, 1)
                if k == 12:
                    gate_output(0, 0)
                if k == 13:
                    gate_output(0, 1, bank=first_banks[1])
                if k == 14:
                    dve.wait_ge(acc_by_pool, 1)
                    gate_output(0, 2, bank=first_banks[2])
                if k == 15:
                    add_output(0, 2)
            dve.wait_ge(acc_by_pool, 2)
            with dve.Fori(1, 3) as i:
                for k in range(PASS):
                    unit(i, k)
                    group_end(i, k)
            for k in range(PASS):
                unit(3, k, split_next=k < UNITS)
                group_end(3, k)
            dve.wait_ge(layer2_done, 4 * PASS)
            for j in range(2):
                c = slice(j * T, (j + 1) * T)
                nc.vector.scalar_tensor_tensor(gated[1][:, c], ps_out[1][:, c], par[:, EXP_B2 + E - 1:EXP_B2 + E],
                                               gate_all[1][:, HALF + j * T:HALF + (j + 1) * T], ALU.add, ALU.mult).then_inc(last_gated, 1)

        @block.tensor
        def _(pe):
            def x_transposes(*tiles):
                for t in tiles:
                    n, j = t // TH, t % TH
                    if j == 0:
                        pe.wait_ge(x_in[n], 16)
                    ins = nc.tensor.transpose(ps_aux[n][:, j * P:(j + 1) * P], x_tok[:, t, :], ident)
                    if j == TH - 1:
                        ins.then_inc(pe_x, 1)

            def z_transposes(b):
                if b < B - 1:
                    pe.wait_ge(z_done, b + 1)
                else:
                    pe.wait_ge(z_by_pool, 1)
                for j in range(2):
                    ins = nc.tensor.transpose(ps_z[b][:, j * P:(j + 1) * P], z_tok[:, 2 * b + j, :], ident)
                ins.then_inc(pe_z, 1)

            def keep_warm(count):
                for _ in range(count):
                    nc.tensor.matmul(ps_out[0][:], w1(w_hi[0], 0), w_hi[0][:, 0:HALF], start=True, stop=True)

            def mlp(k, rows, weight, moving, need):
                if need:
                    pe.wait_ge(mlp_copied, need)
                nc.tensor.matmul(ps_hid[k // 5][0:rows, 8 * k:8 * k + B], weight, moving, start=True, stop=True).then_inc(pe_mlp, 1)

            def split_product(out_, hi, lo, moving_hi, moving_lo, start, stop, half_ready=None):
                nc.tensor.matmul(out_, hi, moving_hi, start=start, stop=False)
                nc.tensor.matmul(out_, lo, moving_hi, start=False, stop=False)
                if half_ready:
                    pe.wait_ge(x_lo_done, half_ready)
                return nc.tensor.matmul(out_, hi, moving_lo, start=False, stop=stop)

            def logits_of(n):
                pe.wait_ge(scaled_done, 2 * n + 2)
                for t in range(n * TH, (n + 1) * TH):
                    ins = nc.tensor.matmul(ps_out[1][:, t * E:(t + 1) * E], scaled[:, t * P:(t + 1) * P], par[:, ROUTER:ROUTER + E],
                                           start=True, stop=True)
                ins.then_inc(pe_logits, 1)

            def gate_transposes():
                pe.wait_ge(combine_done, 1)
                nc.tensor.transpose(ps_aux[0][0:E * NT, 0:P], combine[:].rearrange("p e t -> p (e t)"), ident).then_inc(pe_gates, 1)

            def layer1(i, k, first=False):
                kk = k % PASS
                s, n, c, q = kk // UNITS, kk // C % 2, kk % C, kk % 4
                u = PASS * i + k
                if kk % UNITS == 0:
                    if first and k < PASS:
                        pe.wait_ge(w_lo_first, s + 1)
                    else:
                        pe.wait_ge(w_lo_done, 2 * i + k // UNITS - 1)
                if first and k in (0, 4):
                    pe.wait_ge(x_hi_done, k // 2 + 2)
                if not (first and k < 4):
                    pe.wait_ge(act_done, u - 3)
                split_product(ps_hid[q][:], w1(w_hi[s], c), w1(w_lo[s], c), half(x_hi, n), half(x_lo, n), True, True,
                              half_ready=n + 1 if first and k in (0, 4) else None).then_inc(layer1_done, 1)

            def layer2(i, k, first=False):
                s, n, c, q = k // UNITS, k // C % 2, k % C, k % 4
                pe.wait_ge(lo_done, PASS * i + k + 1)
                bank = first_banks[k // C] if first else ps_out[n]
                if c == 0 and not first:
                    pe.wait_ge(gated_done, 4 * i + k // C - 1)
                split_product(bank[:], w2(w_hi[s], c), w2(w_lo[s], c), hid_hi[q][:], hid_lo[q][:], c == 0, c == C - 1).then_inc(layer2_done, 1)

            def final(n, last):
                src = gated[1] if last else acc[n]
                if not last:
                    pe.wait_ge(rotation_done, 1)
                    pe.wait_ge(act_done, E * UNITS)
                    pe.wait_ge(acc_done, 13 - n)
                for j in range(TH):
                    b = (n * TH + j) // 2
                    if last and j % 2 == 0:
                        pe.wait_ge(last_gated, j // 2 + 1)
                    ins = nc.tensor.matmul(ps_final[n][j // 2][:, j % 2 * D:(j % 2 + 1) * D], src[:, j * P:(j + 1) * P],
                                           rotation[:, b, :], start=n == 0 or not last and j % 2 == 0,
                                           stop=last or n == 0, skip_group_check=n == 1)
                    if j % 2 and (last or n == 0):
                        ins.then_inc(pe_final, 1)

            pe.wait_ge(onehot_done, 1)
            pe.wait_ge(sub_in, 16)
            mlp(0, SE, sub[0:SUBJECTS, SUBJ:SUBJ + SE], onehot[:], 0)
            mlp(1, SH, sub[0:SE, HYP_W1:HYP_W1 + SH], emb[:], 1)
            pe.wait_ge(par_in, 16)
            x_transposes(0, 1)
            mlp(2, SH, sub[:, HYP_W2:HYP_W2 + SH], hyp1[:], 2)
            x_transposes(2, 3)
            z_transposes(0)
            mlp(3, SH // 2, sub[:, STY_W1:STY_W1 + SH // 2], hyp[:], 3)
            z_transposes(1)
            x_transposes(4)
            mlp(4, P, sub[0:SH // 2, STY_W2:STY_W2 + D], sty1[:], 4)
            mlp(5, P, sub[0:SH // 2, STY_W2 + D:STY_W2 + 2 * D], sty1[:], 4)
            pe.wait_ge(w_hi0_done, 1)
            pe.wait_ge(h_done, 1)
            x_transposes(5, 6, 7)
            keep_warm(2)
            z_transposes(2)
            keep_warm(3)
            z_transposes(3)
            pe.wait_ge(mlp_copied, 6)
            for k in range(AHEAD):
                if k == 2:
                    pe.wait_ge(h_done, B)
                layer1(0, k, first=True)
                if k == 1:
                    logits_of(0)
            for k in range(PASS):
                layer1(0, k + AHEAD, first=True)
                if k == 0:
                    logits_of(1)
                if k == C:
                    pe.wait_ge(x_copied, 2)
                if k == 2 * C:
                    pe.wait_ge(gates_copied, 1)
                if k == 3 * C:
                    pe.wait_ge(logits_copied, 1)
                layer2(0, k, first=True)
                if k == 5:
                    pe.wait_ge(x_copied, 1)
                    gate_transposes()
            with pe.Fori(1, 3) as i:
                for k in range(PASS):
                    layer1(i, k + AHEAD)
                    layer2(i, k)
            for k in range(PASS):
                if k + AHEAD < PASS:
                    layer1(3, k + AHEAD)
                layer2(3, k)
                if k == PASS - 2:
                    final(1, False)
            final(0, False)
            final(1, True)


def _pack(inputs):
    import numpy as np

    f = {k: np.asarray(v) for k, v in inputs.items()}
    g = lambda name: f["L0_cond_" + name]
    params = np.zeros((P, NPAR), np.float32)
    params[:, IDENT:IDENT + P] = np.eye(P)
    for d in range(P):
        params[d, PARTNER + (d ^ 1)] = 1.0 if d % 2 else -1.0
    for col, name in ((LN_G, "ln_g"), (LN_B, "ln_b"), (HYP_B1, "hyp_b1"), (HYP_B2, "hyp_b2")):
        params[:, col] = g(name)
    params[:SH // 2, STY_B1] = g("sty_b1")
    params[:, STY_BG] = g("sty_b2")[:D]
    params[:, STY_BB] = g("sty_b2")[D:]
    for d in range(P):
        params[d, ANGLE:ANGLE + B] = f["condB_theta"] if d % 4 < 2 else f["condB_phi"]
    params[:, ROUTER:ROUTER + E] = g("router_w")
    params[:, EXP_B2:EXP_B2 + E] = g("exp_b2").T
    params[:, EXPERT_NO:EXPERT_NO + E] = np.arange(E)
    subnet = np.zeros((P, NSUB), np.float32)
    subnet[:, HYP_W2:HYP_W2 + SH] = g("hyp_w2")
    subnet[:, STY_W1:STY_W1 + SH // 2] = g("sty_w1")
    subnet[:SE, HYP_W1:HYP_W1 + SH] = g("hyp_w1")
    subnet[:SH // 2, STY_W2:STY_W2 + 2 * D] = g("sty_w2")
    subnet[:SUBJECTS, SUBJ:SUBJ + SE] = g("subj_emb")
    w1 = g("exp_w1")
    w2 = g("exp_w2").reshape(E, C, P, D).transpose(0, 2, 1, 3).reshape(E, P, C * D)
    experts = np.ascontiguousarray(np.concatenate([w1, w2], axis=2))
    biases = g("exp_b1").reshape(E, C, P).transpose(0, 2, 1)
    return {"x": np.ascontiguousarray(f["x"]), "itok": np.ascontiguousarray(f["itok_B_6_14"]), "params": params,
            "subnet": subnet, "experts": experts, "biases": np.ascontiguousarray(biases)}


def kernel(**inputs):
    import numpy as np
    import concourse.bacc as bacc
    from concourse.bass_utils import run_bass_kernel_spmd

    nc = bacc.Bacc("TRN2", target_bir_lowering=False, num_devices=1)
    arrays, args = {}, {}
    for name, a in _pack(inputs).items():
        arrays["in_" + name] = a
        args[name] = nc.dram_tensor("in_" + name, a.shape, mybir.dt.from_np(a.dtype), kind="ExternalInput").ap()
    args["out"] = nc.dram_tensor("out_y", (B, T, D), mybir.dt.from_np(np.dtype("float32")), kind="ExternalOutput").ap()
    moe_rotate(nc, **args)
    r = run_bass_kernel_spmd(nc, [arrays], core_ids=[0])
    return r.results[0]["out_y"]
```
